# Optimizing a Trainium2 kernel written in Bass

```python
import numpy as np
import jax
import jax.numpy as jnp

def _softmax(x, axis=-1):
    return jax.nn.softmax(x, axis=axis)

def _gelu(x):
    return jax.nn.gelu(x, approximate=True)

def _silu(x):
    return jax.nn.silu(x)

def _sigmoid(x):
    return jax.nn.sigmoid(x)

def _layernorm(x, axis=-1, eps=1e-05):
    m = jnp.mean(x, axis=axis, keepdims=True)
    v = jnp.var(x, axis=axis, keepdims=True)
    return (x - m) / jnp.sqrt(v + eps)

def _scatter_add(tgt, idx, src, axis=0):
    return tgt.at[idx].add(src)

def _segment_sum(src, seg, n):
    return jax.ops.segment_sum(src, seg, n)
kernel_name = 'mk_sandwich_d1_jaxref_r4_c14b80'

def setup_inputs(seed: int=0):
    np.random.seed(seed)
    _w = jnp.asarray

    def _L0_attn_setup():
        import jax, jax.numpy as jnp
        import numpy as np
        D_MODEL = 256
        N_HEADS = 16
        HEAD_DIM = D_MODEL // N_HEADS
        MAX_LEN = 512
        BATCH = 2
        SEQ = 512
        key = jax.random.key(seed)
        ks = jax.random.split(key, 10)
        s = 1.0 / np.sqrt(D_MODEL)
        inp = {'x': jax.random.normal(ks[0], (BATCH, SEQ, D_MODEL), dtype=jnp.float32), 'Wq': jax.random.uniform(ks[1], (D_MODEL, D_MODEL), jnp.float32, -s, s), 'bq': jax.random.uniform(ks[2], (D_MODEL,), jnp.float32, -s, s), 'Wk': jax.random.uniform(ks[3], (D_MODEL, D_MODEL), jnp.float32, -s, s), 'bk': jax.random.uniform(ks[4], (D_MODEL,), jnp.float32, -s, s), 'Wv': jax.random.uniform(ks[5], (D_MODEL, D_MODEL), jnp.float32, -s, s), 'bv': jax.random.uniform(ks[6], (D_MODEL,), jnp.float32, -s, s), 'Wo': jax.random.uniform(ks[7], (D_MODEL, D_MODEL), jnp.float32, -s, s), 'bo': jax.random.uniform(ks[8], (D_MODEL,), jnp.float32, -s, s), 'rel_emb': jax.random.normal(ks[9], (MAX_LEN * 2 - 1, HEAD_DIM), dtype=jnp.float32)}
        return inp
    _L0_attn_in = _L0_attn_setup()

    def _L0_ffn_setup():
        import jax, jax.numpy as jnp
        import numpy as np
        B, S, D = (8, 1024, 256)
        E, R, K = (6, 16, 2)
        key = jax.random.key(seed)
        ks = jax.random.split(key, 9)
        sc = 0.02
        return {'x': jax.random.normal(ks[0], (B, S, D), jnp.float32), 'base_W': jax.random.normal(ks[1], (D, D), jnp.float32) * sc, 'base_b': jax.random.normal(ks[2], (D,), jnp.float32) * sc, 'shared_A': jax.random.normal(ks[3], (R, D), jnp.float32) * sc, 'shared_B': jax.random.normal(ks[4], (D, R), jnp.float32) * sc, 'routed_A': jax.random.normal(ks[5], (E, R, D), jnp.float32) * sc, 'routed_B': jax.random.normal(ks[6], (E, D, R), jnp.float32) * sc, 'router_W': jax.random.normal(ks[7], (E, D), jnp.float32) * sc, 'router_b': jax.random.normal(ks[8], (E,), jnp.float32) * sc}
    _L0_ffn_in = _L0_ffn_setup()
    _d = {'L0_attn_x': _L0_attn_in['x'], 'L0_attn_Wq': _L0_attn_in['Wq'], 'L0_attn_bq': _L0_attn_in['bq'], 'L0_attn_Wk': _L0_attn_in['Wk'], 'L0_attn_bk': _L0_attn_in['bk'], 'L0_attn_Wv': _L0_attn_in['Wv'], 'L0_attn_bv': _L0_attn_in['bv'], 'L0_attn_Wo': _L0_attn_in['Wo'], 'L0_attn_bo': _L0_attn_in['bo'], 'L0_attn_rel_emb': _L0_attn_in['rel_emb'], 'L0_ffn_base_W': _L0_ffn_in['base_W'], 'L0_ffn_base_b': _L0_ffn_in['base_b'], 'L0_ffn_shared_A': _L0_ffn_in['shared_A'], 'L0_ffn_shared_B': _L0_ffn_in['shared_B'], 'L0_ffn_routed_A': _L0_ffn_in['routed_A'], 'L0_ffn_routed_B': _L0_ffn_in['routed_B'], 'L0_ffn_router_W': _L0_ffn_in['router_W'], 'L0_ffn_router_b': _L0_ffn_in['router_b']}
    _x0 = _d['L0_attn_x']
    _d['L0_attn_x'] = jax.random.normal(jax.random.fold_in(jax.random.key(seed), 1), (16, 1024, 256), dtype=_x0.dtype)
    del _x0
    return _d

def reference(L0_attn_x, L0_attn_Wq, L0_attn_bq, L0_attn_Wk, L0_attn_bk, L0_attn_Wv, L0_attn_bv, L0_attn_Wo, L0_attn_bo, L0_attn_rel_emb, L0_ffn_base_W, L0_ffn_base_b, L0_ffn_shared_A, L0_ffn_shared_B, L0_ffn_routed_A, L0_ffn_routed_B, L0_ffn_router_W, L0_ffn_router_b):

    def _L0_attn_ref(x, Wq, bq, Wk, bk, Wv, bv, Wo, bo, rel_emb):
        import jax, jax.numpy as jnp
        import numpy as np
        D_MODEL = 256
        N_HEADS = 16
        HEAD_DIM = D_MODEL // N_HEADS
        MAX_LEN = 512
        BATCH = 2
        SEQ = 512
        B, L, _ = x.shape

        def lin(x, W, b):
            return jnp.einsum('bld,ed->ble', x, W) + b

        def split_heads(t):
            return t.reshape(B, L, N_HEADS, HEAD_DIM).transpose(0, 2, 1, 3)
        q = split_heads(lin(x, Wq, bq))
        k = split_heads(lin(x, Wk, bk))
        v = split_heads(lin(x, Wv, bv))
        r = jnp.arange(L)
        idx = r[None, :] - r[:, None] + (MAX_LEN - 1)
        rel = rel_emb[idx]
        qk = jnp.einsum('bhld,bhrd->bhlr', q, k) / np.sqrt(HEAD_DIM)
        qk = qk + jnp.einsum('bhld,lrd->bhlr', q, rel)
        att = jax.nn.softmax(qk, axis=-1)
        out = jnp.einsum('bhlr,bhrd->bhld', att, v)
        out = out.transpose(0, 2, 1, 3).reshape(B, L, D_MODEL)
        return lin(out, Wo, bo)

    def _L0_ffn_ref(x, base_W, base_b, shared_A, shared_B, routed_A, routed_B, router_W, router_b):
        import jax, jax.numpy as jnp
        import numpy as np
        B, S, D = (8, 1024, 256)
        E, R, K = (6, 16, 2)
        base_out = jax.lax.stop_gradient(jnp.einsum('bsi,oi->bso', x, base_W) + base_b)
        shared_out = jnp.einsum('bsr,or->bso', jnp.einsum('bsi,ri->bsr', x, shared_A), shared_B)
        logits = jnp.einsum('bsi,ei->bse', x, router_W) + router_b
        gate = jax.nn.softmax(logits, axis=-1)
        topk_w, topk_i = jax.lax.top_k(gate, K)
        sparse_w = jnp.sum(jax.nn.one_hot(topk_i, E, dtype=gate.dtype) * topk_w[..., None], axis=-2)
        sparse_w = sparse_w / (jnp.sum(sparse_w, axis=-1, keepdims=True) + 1e-06)
        h = jnp.einsum('bsi,eri->bser', x, routed_A)
        routed_outs = jnp.einsum('bser,eor->bseo', h, routed_B)
        routed_out = jnp.einsum('bseo,bse->bso', routed_outs, sparse_w)
        return base_out + shared_out + routed_out
    x = L0_attn_x
    x = x + _layernorm(_L0_attn_ref(_layernorm(x, axis=-1), L0_attn_Wq, L0_attn_bq, L0_attn_Wk, L0_attn_bk, L0_attn_Wv, L0_attn_bv, L0_attn_Wo, L0_attn_bo, L0_attn_rel_emb), axis=-1)
    x = x + _layernorm(_L0_ffn_ref(_layernorm(x, axis=-1), L0_ffn_base_W, L0_ffn_base_b, L0_ffn_shared_A, L0_ffn_shared_B, L0_ffn_routed_A, L0_ffn_routed_B, L0_ffn_router_W, L0_ffn_router_b), axis=-1)
    return x

_drawn_inputs = setup_inputs


def setup_inputs(seed=0):
    import zlib

    import numpy as np

    out = dict(_drawn_inputs(seed))
    spreads = {}
    factors = {}
    for name, (base, spread) in spreads.items():
        noise = np.random.default_rng([zlib.crc32(name.encode()), seed]).standard_normal(out[name].shape)
        drawn = base * np.exp(spread * noise) if base else spread * noise
        out[name] = jnp.asarray(drawn.astype(out[name].dtype))
    for name, factor in factors.items():
        out[name] = (out[name] * factor).astype(out[name].dtype)
    return out
```

```python
from contextlib import ExitStack

import numpy as np

import concourse.bass as bass
from concourse import mybir

B, L, D = 16, 1024, 256
H, HD = 16, 16
MAX_LEN = 512
NREL = 2 * MAX_LEN - 1
E, R = 6, 16
P = 128
NT = B * L // P
TPB = L // P
JC = L // P
NJP = JC // 2
IW = 32
NI = P // IW
NG = NJP * NI
ROWS = 96
SPLIT = (0, 0, 1)
SPLIT_ST = (0, 1, 0)
TWC = 3 * P
NU = 2 * L
NA = R + E * R
NH = NA + E
EPS = 1e-5
RING = [0, 1, 2] * 4 + [0, 1, 0, 2]
DIST = []
for _g in range(NG):
    _d = 1
    while RING[(_g - _d) % NG] != RING[_g]:
        _d += 1
    DIST.append(_d)


def sandwich_kernel(nc, x, wqT, bq, wkT, bk, wvT, bv, woT, bo, relT, baseT, base_b,
                    shAT, shBT, roAT, roBT, rtT, rtb, out):
    f32, f16 = mybir.dt.float32, mybir.dt.float16
    ALU = mybir.AluOpType
    ACT = mybir.ActivationFunctionType
    AX = mybir.AxisListType

    qk_s = nc.dram_tensor("qk_s", (2, 2, B + 1, D, L), f16, kind="Internal").ap()
    v_s = nc.dram_tensor("v_s", ((B + 1) * TPB, P, H * 32), f32, kind="Internal").ap()
    t_s = nc.dram_tensor("t_s", (2, HD, NU + 1), f16, kind="Internal").ap()
    tw_s = nc.dram_tensor("tw_s", (ROWS, NU), f16, kind="Internal").ap()

    ctx = ExitStack()
    with ctx:
        def sb(name, shape, dt=f32):
            return ctx.enter_context(nc.sbuf_tensor(name, shape, dt))

        def sem(name):
            return ctx.enter_context(nc.semaphore(name))

        ident = sb("ident", [P, P])
        ident16 = sb("ident16", [H, H], f16)
        ones16 = sb("ones16", [P, P], f16)
        mask_h = sb("mask_h", [H, H, IW], f16)
        mask_q = sb("mask_q", [ROWS, H, IW], f16)
        mask_r = sb("mask_r", [ROWS, H, IW], f16)
        tri = sb("tri", [P, E, E])
        mhalf = sb("mhalf", [P, 1])
        eps = sb("eps", [P, 1])
        one = sb("one", [P, 1])
        w_q = sb("w_q", [P, 2, D])
        w_k = sb("w_k", [P, 2, D])
        w_v = sb("w_v", [P, 2, D])
        w_o = sb("w_o", [P, 2, D])
        w_base = sb("w_base", [P, 2, D])
        w_a = sb("w_a", [P, 2, NH])
        w_b = sb("w_b", [NA, D])
        b_qk = sb("b_qk", [P, 4])
        b_v = sb("b_v", [P, D])
        b_o = sb("b_o", [P, D])
        b_base = sb("b_base", [P, D])
        b_rt = sb("b_rt", [P, E])
        relf = sb("relf", [HD, NREL])
        tf = sb("tf", [HD, NU + 1])
        th = sb("th", [HD, NU + 1], f16)
        tl = sb("tl", [HD, NU + 1], f16)
        tw = sb("tw", [ROWS, NJP, TWC], f16)
        ks = sb("ks", [ROWS, H // 2, L], f16)
        vs = sb("vs", [P, JC, H, 32])
        raw = sb("raw", [ROWS, H, P], f16)
        qm = sb("qm", [ROWS, NI, H, IW], f16)
        rm = sb("rm", [ROWS, NI, IW // 2, H, 2], f16)
        prob = sb("prob", [P, 2, 2, H, P])
        r1 = sb("r1", [P, 2 * H])
        r2 = sb("r2", [P, H])
        nm = sb("nm", [H, 2, P], f16)
        nmm = sb("nmm", [P, H, IW], f16)
        ot = sb("ot", [P, 4, P])
        parts = sb("parts", [P, NJP, H, 17])
        nmt = sb("nmt", [P, NJP, H])
        nmin = sb("nmin", [P, H])
        dm = sb("dm", [P, NJP, H])
        wst = sb("wst", [P, NJP, H])
        wp = sb("wp", [P, NJP, H, 17])
        osum = sb("osum", [P, H, 17])
        rden = sb("rden", [P, H])
        o = sb("o", [P, H, HD])
        oT = sb("oT", [P, 2, P])
        xin = sb("xin", [P, D])
        xn = sb("xn", [P, D])
        xT = sb("xT", [P, 2, P])
        st0 = sb("st0", [P, 6])
        mv0 = sb("mv0", [P, 2])
        ve0 = sb("ve0", [P, 1])
        rs0 = sb("rs0", [P, 1])
        qkf = sb("qkf", [P, 4, P])
        qkh = sb("qkh", [P, 4, P], f16)
        qkl = sb("qkl", [P, 4, P], f16)
        vpad = sb("vpad", [P, H, 32])
        xr = sb("xr", [P, D])
        y0 = sb("y0", [P, D])
        y = sb("y", [P, D])
        yn = sb("yn", [P, D])
        x1 = sb("x1", [P, D])
        x1b = sb("x1b", [P, D])
        xn1 = sb("xn1", [P, D])
        x1T = sb("x1T", [P, 2, P])
        st1 = sb("st1", [P, 6])
        mv1 = sb("mv1", [P, 2])
        ve1 = sb("ve1", [P, 1])
        rs1 = sb("rs1", [P, 1])
        st2 = sb("st2", [P, 6])
        mv2 = sb("mv2", [P, 2])
        ve2 = sb("ve2", [P, 1])
        rs2 = sb("rs2", [P, 1])
        st3 = sb("st3", [P, 6])
        mv3 = sb("mv3", [P, 2])
        ve3 = sb("ve3", [P, 1])
        rs3 = sb("rs3", [P, 1])
        hf = sb("hf", [P, NH])
        lg = sb("lg", [P, E])
        nlm = sb("nlm", [P, 1])
        eg = sb("eg", [P, E])
        gsum = sb("gsum", [P, 1])
        rg = sb("rg", [P, 1])
        gate = sb("gate", [P, E])
        cgt = sb("cgt", [P, E, E])
        ceq = sb("ceq", [P, E, E])
        ceqt = sb("ceqt", [P, E, E])
        cadd = sb("cadd", [P, E, E])
        rank = sb("rank", [P, E])
        sw = sb("sw", [P, E])
        ssum = sb("ssum", [P, 1])
        ssume = sb("ssume", [P, 1])
        rss = sb("rss", [P, 1])
        swn = sb("swn", [P, E])
        hw = sb("hw", [P, NA])
        hT = sb("hT", [NA, P])
        y20 = sb("y20", [P, D])
        y2 = sb("y2", [P, D])
        y2n = sb("y2n", [P, D])
        res = sb("res", [P, D])

        sc = ctx.enter_context(nc.psum_tensor("sc", [P, 6, 512], f32))
        pw = ctx.enter_context(nc.psum_tensor("pw", [P, 512], f32))
        pm = ctx.enter_context(nc.psum_tensor("pm", [P, 512], f32))
        p_max = pm[0:H, 0:P]
        p_n = pm[:, P:2 * P]
        p_t = pm[:, 2 * P:4 * P]

        s_const = sem("s_const")
        s_cpool = sem("s_cpool")
        s_cdve = sem("s_cdve")
        s_tsplit = sem("s_tsplit")
        s_tst = sem("s_tst")
        s_tws = sem("s_tws")
        s_tw = [sem(f"s_tw{j}") for j in range(NJP)]
        s_ks = [sem(f"s_ks{j}") for j in range(NJP)]
        s_vs = [sem(f"s_vs{j}") for j in range(NJP)]
        s_raw = sem("s_raw")
        s_mask = sem("s_mask")
        s_scores = sem("s_scores")
        s_rmax = sem("s_rmax")
        s_maxT = sem("s_maxT")
        s_nm = sem("s_nm")
        s_shift = sem("s_shift")
        s_exp = sem("s_exp")
        s_pv = sem("s_pv")
        s_ot = sem("s_ot")
        s_ott = sem("s_ott")
        s_part = sem("s_part")
        s_dm = sem("s_dm")
        s_wst = sem("s_wst")
        s_wp = sem("s_wp")
        s_osum = sem("s_osum")
        s_o = sem("s_o")
        s_oTp = sem("s_oTp")
        s_oT = sem("s_oT")
        s_wo = sem("s_wo")
        s_y0 = sem("s_y0")
        s_nmtp = sem("s_nmtp")
        s_nmt = sem("s_nmt")
        s_mv1 = sem("s_mv1")
        s_rs1 = sem("s_rs1")
        s_xr = sem("s_xr")
        s_x1 = sem("s_x1")
        s_mv2 = sem("s_mv2")
        s_rs2 = sem("s_rs2")
        s_xn1 = sem("s_xn1")
        s_x1Tp = sem("s_x1Tp")
        s_x1T = sem("s_x1T")
        s_x1b = sem("s_x1b")
        s_hp = sem("s_hp")
        s_hf = sem("s_hf")
        s_lg = sem("s_lg")
        s_eg = sem("s_eg")
        s_hw = sem("s_hw")
        s_hTp = sem("s_hTp")
        s_hT = sem("s_hT")
        s_y2p = sem("s_y2p")
        s_y20 = sem("s_y20")
        s_mv3 = sem("s_mv3")
        s_rs3 = sem("s_rs3")
        s_res = sem("s_res")
        s_out = sem("s_out")
        s_x = sem("s_x")
        s_mv0 = sem("s_mv0")
        s_rs0 = sem("s_rs0")
        s_xn = sem("s_xn")
        s_xTp = sem("s_xTp")
        s_xT = sem("s_xT")
        s_qkp = sem("s_qkp")
        s_qkf = sem("s_qkf")
        s_qks = sem("s_qks")
        s_qkst = sem("s_qkst")
        s_vp = sem("s_vp")
        s_v = sem("s_v")
        s_vst = sem("s_vst")
        s_step = sem("s_step")

        N_CONST = 20 * 16
        block = ctx.enter_context(nc.Block())

        def batch_of(t):
            return t // TPB

        def passes(eng, tile):
            tile(-TPB, 0, att=False, proj=True, a=False, b=False)
            with eng.Fori(1, TPB) as n:
                tile(n - TPB, n, att=False, proj=True, a=False, b=False)
            tile(0, TPB, att=True, proj=True, a=False, b=False)
            tile(1, TPB + 1, att=True, proj=True, a=True, b=False)
            with eng.Fori(2, NT) as t:
                tile(t, t + TPB, att=True, proj=True, a=True, b=True)
            tile(NT, None, att=False, proj=False, a=True, b=True)
            tile(NT + 1, None, att=False, proj=False, a=False, b=True)

        @block.sync
        def _(sp):
            def const(dst, src):
                sp.dma_start(dst, src).then_inc(s_const, 16)

            def two(a):
                return a.rearrange("(c p) n -> p c n", p=P)

            sp.sem_inc(s_out, 16)
            const(relf[:, :], relT)
            for dst, src in ((w_q, wqT), (w_k, wkT), (w_v, wvT), (w_o, woT), (w_base, baseT)):
                const(dst[:, :, :], two(src))
            const(w_a[:, :, 0:R], two(shAT))
            const(w_a[:, :, R:NA], two(roAT))
            const(w_a[:, :, NA:NH], two(rtT))
            const(w_b[0:R, :], shBT)
            const(w_b[R:NA, :], roBT)
            for c in range(2):
                const(b_qk[:, c:c + 1], bq[c * P:(c + 1) * P].rearrange("(p a) -> p a", a=1))
                const(b_qk[:, 2 + c:3 + c], bk[c * P:(c + 1) * P].rearrange("(p a) -> p a", a=1))
            for dst, src in ((b_v, bv), (b_o, bo), (b_base, base_b), (b_rt, rtb)):
                const(dst[:, :], src.rearrange("(a n) -> a n", a=1).to_broadcast((P, src.shape[0])))
            const(xin[:, :], x[0:P, :])
            assert N_CONST == 16 * 20

            sp.wait_ge(s_tsplit, 2)
            sp.dma_start(t_s[0], th[:, :]).then_inc(s_tst, 16)
            sp.dma_start(t_s[1], tl[:, :]).then_inc(s_tst, 16)
            sp.wait_ge(s_tst, 32)
            for s in range(2):
                for k, part in enumerate(SPLIT_ST):
                    r = (3 * s + k) * HD
                    sp.dma_start(tw_s[r:r + HD, :], t_s[part, :, 1 - s:1 - s + NU]).then_inc(s_tws, 16)
            sp.wait_ge(s_tws, 6 * 16)

            def load_window(it, jp):
                u = (TPB - 1) * P - it * P + 2 * P * jp
                sp.dma_start(tw[:, jp, :], tw_s[:, bass.ds(u, TWC)] if not isinstance(u, int)
                             else tw_s[:, u:u + TWC]).then_inc(s_tw[jp], 16)

            def load_raw(b, it):
                for s in range(2):
                    for k, part in enumerate(SPLIT):
                        r = (3 * s + k) * HD
                        src = qk_s[part, 0, b].rearrange("(h d) t -> d h t", d=HD)
                        sp.dma_start(raw[r:r + HD, :, :], src[:, :, it * P:it * P + P] if isinstance(it, int)
                                     else src[:, :, bass.ds(it * P, P)]).then_inc(s_raw, 16)

            def load_keys(b, jp):
                for s in range(2):
                    for k, part in enumerate(SPLIT_ST):
                        r = (3 * s + k) * HD
                        src = qk_s[part, 1, b].rearrange("(h s d) t -> s d h t", s=2, d=HD)
                        j = 2 * P * jp
                        sp.dma_start(ks[r:r + HD, :, j:j + 2 * P], src[s, :, :, j:j + 2 * P])\
                          .then_inc(s_ks[jp], 16)

            def load_values(b, jp):
                n = b * TPB + 2 * jp
                src = v_s[n:n + 2] if isinstance(n, int) else v_s[bass.ds(n, 2)]
                sp.dma_start(vs[:, 2 * jp:2 * jp + 2, :, :].rearrange("p c h d -> p c (h d)"),
                             src.rearrange("c p f -> p c f")).then_inc(s_vs[jp], 16)

            def after(sem, value):
                sp.wait_ge(sem, value)
                sp.sem_inc(s_step, 1)

            def tile(b, it, att, proj, a, bb, new=False, last=False, end=False, wrap=False, first=False):
                t = b * TPB + it
                n = t + TPB
                if att:
                    if not first:
                        after(s_scores, t * NG)
                        load_window(it, NJP - 1)
                        if new:
                            after(s_qkst, n * 64)
                            load_keys(b, NJP - 1)
                    after(s_mask, t * NI + NI)
                    if last:
                        load_raw(b + 1, 0)
                    else:
                        load_raw(b, it + 1)
                if a:
                    after(s_x1, t - 1)
                    row = (t - 1) * P
                    sp.dma_start(xr[:, :], x[row:row + P, :] if isinstance(row, int)
                                 else x[bass.ds(row, P), :]).then_inc(s_xr, 16)
                if new:
                    after(s_pv, t * NJP)
                    after(s_vst, n * 16)
                    load_values(b, NJP - 1)
                if att and not end:
                    nit = 0 if last else it + 1
                    after(s_scores, t * NG + NI)
                    load_window(nit, 0)
                    if last:
                        load_keys(b + 1, 0)
                if proj:
                    after(s_xn, n + 1)
                    row = 0 if wrap and last else (it + 1) * P if wrap else (n + 1) * P
                    sp.dma_start(xin[:, :], x[row:row + P, :] if isinstance(row, int)
                                 else x[bass.ds(row, P), :]).then_inc(s_x, 16)
                if last and not end:
                    after(s_pv, t * NJP + 1)
                    load_values(b + 1, 0)
                if att and not end:
                    after(s_scores, t * NG + 2 * NI)
                    load_window(nit, 1)
                    if last:
                        load_keys(b + 1, 1)
                if proj:
                    after(s_qks, n + 1)
                    for part, src in ((0, qkh), (1, qkl)):
                        for sel in range(2):
                            dst = qk_s[part, sel, b + 1].rearrange("(c p) t -> p c t", p=P)
                            sp.dma_start(dst[:, :, it * P:it * P + P] if isinstance(it, int)
                                         else dst[:, :, bass.ds(it * P, P)],
                                         src[:, 2 * sel:2 * sel + 2, :]).then_inc(s_qkst, 16)
                if last and not end:
                    after(s_pv, t * NJP + 2)
                    load_values(b + 1, 1)
                if att and not end:
                    after(s_scores, t * NG + 3 * NI)
                    load_window(nit, 2)
                    if last:
                        load_keys(b + 1, 2)
                if proj:
                    after(s_v, n + 1)
                    dst = v_s[n] if isinstance(n, int) else v_s[bass.ds(n, 1)].rearrange("a p f -> (a p) f")
                    sp.dma_start(dst, vpad[:, :, :].rearrange("p h d -> p (h d)")).then_inc(s_vst, 16)
                if last and not end:
                    after(s_pv, t * NJP + 3)
                    load_values(b + 1, 2)
                if bb:
                    after(s_res, t - 1)
                    row = (t - 2) * P
                    sp.dma_start(out[row:row + P, :] if isinstance(row, int)
                                 else out[bass.ds(row, P), :], res[:, :]).then_inc(s_out, 16)

            tile(-1, 0, False, True, False, False)
            with sp.Fori(1, TPB) as it:
                tile(-1, it, False, True, False, False)
            sp.wait_ge(s_qkst, TPB * 64)
            sp.wait_ge(s_vst, TPB * 16)
            load_raw(0, 0)
            for jp in range(NJP):
                load_window(0, jp)
                load_keys(0, jp)
                load_values(0, jp)
            tile(0, 0, True, True, False, False, first=True)
            tile(0, 1, True, True, True, False)
            with sp.Fori(2, TPB - 1) as it:
                tile(0, it, True, True, True, True)
            tile(0, TPB - 1, True, True, True, True, last=True)

            def batch(b, wrap=False, turn=False, end=False):
                tile(b, 0, True, True, True, True, new=True, wrap=wrap)
                with sp.Fori(1, TPB - 1) as it:
                    tile(b, it, True, True, True, True, wrap=wrap)
                tile(b, TPB - 1, True, True, True, True, last=True, end=end, wrap=wrap or turn)

            with sp.Fori(1, B - 2) as b:
                batch(b)
            batch(B - 2, turn=True)
            batch(B - 1, wrap=True, end=True)
            tile(B, 0, False, False, True, True)
            tile(B, 1, False, False, False, True)
            sp.wait_ge(s_out, NT * 16 + 16)
            sp.wait_ge(s_x, (NT + TPB) * 16)
            sp.wait_ge(s_qkst, (NT + TPB) * 64)
            sp.wait_ge(s_vst, (NT + TPB) * 16)

        @block.gpsimd
        def _(pool):
            g = nc.gpsimd
            g.memset(ident[:, :], 1.0)
            g.memset(ident16[:, :], 1.0)
            g.memset(ones16[:, :], 1.0)
            g.memset(mask_h[:, :, :], 1.0)
            g.memset(mask_q[:, :, :], 1.0)
            g.memset(mask_r[:, :, :], 1.0)
            g.memset(tri[:, :, :], 1.0)
            g.memset(mhalf[:, :], -0.5)
            g.memset(eps[:, :], EPS)
            g.memset(one[:, :], 1.0)
            g.memset(vpad[:, :, :], 1.0)
            g.memset(nmm[:, :, :], 0.0)
            pool.drain()

            def keep(v, op, base, pattern, mult):
                g.affine_select(out=v, in_=v, compare_op=op, fill=0.0, base=base, pattern=pattern,
                                channel_multiplier=mult)

            keep(ident[:, :], ALU.is_equal, 0, [[-1, P]], 1)
            keep(ident16[:, :], ALU.is_equal, 0, [[-1, H]], 1)
            keep(ones16[:, :], ALU.is_ge, H - 1, [[0, P]], -1)
            keep(mask_h[:, :, :], ALU.is_equal, 0, [[-1, H], [0, IW]], 1)
            half = ROWS // 2
            q4 = mask_q[:, :, :].rearrange("p (h s) i -> p h s i", s=2)
            r4 = mask_r[:, :, :].rearrange("p h (i s) -> p h i s", s=2)
            keep(q4[:, :, 0, :], ALU.is_ge, half - 1, [[0, H // 2], [0, IW]], -1)
            keep(q4[:, :, 1, :], ALU.is_ge, -half, [[0, H // 2], [0, IW]], 1)
            keep(r4[:, :, :, 0], ALU.is_ge, half - 1, [[0, H], [0, IW // 2]], -1)
            keep(r4[:, :, :, 1], ALU.is_ge, -half, [[0, H], [0, IW // 2]], 1)
            keep(tri[:, :, :], ALU.is_gt, 0, [[1, E], [-1, E]], 0)
            pool.drain().then_inc(s_cpool, 1)

            def mask(i):
                src = raw[:, :, i * IW:(i + 1) * IW]
                g.tensor_tensor(qm[:, i, :, :], src, mask_q[:, :, :], ALU.mult)
                g.tensor_tensor(rm[:, i, :, :, :].rearrange("p i h s -> p h i s"),
                                src.rearrange("p h (i s) -> p h i s", s=2),
                                mask_r[:, :, :].rearrange("p h (i s) -> p h i s", s=2),
                                ALU.mult).then_inc(s_mask, 1)

            def rstd(dst, mv, ve):
                g.tensor_tensor(ve[:, :], mv[:, 1:2], eps[:, :], ALU.add)
                pool.drain()
                return g.tensor_tensor(dst[:, :], ve[:, :], mhalf[:, :], ALU.pow)

            def tile(t, n, att, proj, a, b):
                if att:
                    if isinstance(t, int) and t == 0:
                        pool.wait_ge(s_raw, 96)
                        for i in range(NI - 1):
                            mask(i)
                    pool.wait_ge(s_scores, t * NG)
                    mask(NI - 1)
                if b:
                    pool.wait_ge(s_x1, t - 1)
                if proj:
                    pool.wait_ge(s_mv0, n + 1)
                    rstd(rs0, mv0, ve0).then_inc(s_rs0, 1)
                elif b:
                    pool.wait_ge(s_res, t - 2)
                if b:
                    g.tensor_copy(x1b[:, :], x1[:, :]).then_inc(s_x1b, 1)
                if a:
                    pool.wait_ge(s_wst, t)
                    g.tensor_tensor(wp[:, :, :, :].rearrange("p j h d -> p (j h) d"),
                                    parts[:, :, :, :].rearrange("p j h d -> p (j h) d"),
                                    wst[:, :, :].rearrange("p j (h a) -> p (j h) a", a=1)
                                    .to_broadcast((P, NJP * H, 17)), ALU.mult).then_inc(s_wp, 1)
                if proj:
                    pool.wait_ge(s_qkf, n + 1)
                    pool.wait_ge(s_qkst, n * 64)
                    g.tensor_tensor(qkh[:, :, :].rearrange("p c i -> p (c i)"),
                                    qkf[:, :, :].rearrange("p c i -> p (c i)"),
                                    one[:, :].to_broadcast((P, 4 * P)), ALU.mult)
                    pool.drain()
                    g.tensor_tensor(qkl[:, :, :], qkf[:, :, :], qkh[:, :, :], ALU.subtract)\
                     .then_inc(s_qks, 1)
                if a:
                    pool.wait_ge(s_mv1, t)
                    rstd(rs1, mv1, ve1).then_inc(s_rs1, 1)
                if att:
                    pool.wait_ge(s_raw, t * 96 + 192)
                    pool.wait_ge(s_scores, t * NG + NG - NI + 1)
                    mask(0)
                if b:
                    pool.wait_ge(s_mv3, t - 1)
                    rstd(rs3, mv3, ve3).then_inc(s_rs3, 1)
                if a:
                    pool.wait_ge(s_mv2, t)
                    rstd(rs2, mv2, ve2).then_inc(s_rs2, 1)
                if att:
                    for i in range(1, NI - 1):
                        pool.wait_ge(s_scores, t * NG + NG - NI + i + 1)
                        mask(i)

            passes(pool, tile)

        @block.tensor
        def _(pe):
            mm = nc.tensor.matmul
            pe.wait_ge(s_const, N_CONST)
            pe.wait_ge(s_cpool, 1)
            pe.wait_ge(s_cdve, 1)

            def scores(g, c):
                jp, i = divmod(g, NI)
                bank = sc[:, 2 * RING[g] + c, :]
                out3 = bank.rearrange("p (h i) -> p h i", i=IW)
                j = (2 * jp + c) * P
                for h in range(H // 2):
                    last = mm(bank[:, 2 * h * IW:(2 * h + 2) * IW], ks[:, h, j:j + P],
                              qm[:, i, 2 * h:2 * h + 2, :].rearrange("p h i -> p (h i)"),
                              start=(h == 0), stop=False, skip_group_check=True)
                for k in range(IW // 2):
                    u = P - 1 - (i * IW + 2 * k) + c * P
                    last = mm(out3[:, :, 2 * k:2 * k + 2], tw[:, jp, u:u + P], rm[:, i, k, :, :],
                              start=False, stop=False, skip_group_check=True)
                return last

            def transpose_max(g_count):
                pe.wait_ge(s_rmax, g_count)
                nc.tensor.transpose(p_max, r2[:, :], ident[:, :]).then_inc(s_maxT, 1)

            def shift(g, g_count):
                pe.wait_ge(s_nm, g_count)
                for c in range(2):
                    last = mm(sc[:, 2 * RING[g] + c, :], ones16[:, :],
                              nmm[:, :, :].rearrange("p h i -> p (h i)"),
                              start=False, stop=True, skip_group_check=True)
                last.then_inc(s_shift, 1)

            def pv(jp, half):
                for col in (2 * half, 2 * half + 1):
                    for c in range(2):
                        for q in range(4):
                            h = 4 * col + q
                            last = mm(pw[32 * q:32 * q + 32, col * P:(col + 1) * P], vs[:, 2 * jp + c, h, :],
                                      prob[:, jp % 2, c, h, :], start=(c == 0), stop=(c == 1))
                return last

            def transpose_parts(stage):
                pe.wait_ge(s_ot, stage + 1)
                for col in range(4):
                    last = nc.tensor.transpose(pw[:, col * P:(col + 1) * P], ot[:, col, :], ident[:, :])
                last.then_inc(s_ott, 1)

            def transpose2(dst, src):
                for c in range(2):
                    last = nc.tensor.transpose(dst[:, c * P:(c + 1) * P], src[:, c * P:(c + 1) * P],
                                               ident[:, :])
                return last

            def product(dst, lhs, w, more=None):
                for c in range(2):
                    last = mm(dst, lhs[:, c, :], w[:, c, :], start=(c == 0), stop=(c == 1 and more is None))
                if more is not None:
                    last = mm(dst, more[0], more[1], start=False, stop=True)
                return last

            def mixed(t, g, att, a, b):
                jp, k = divmod(g, NI)
                if k == 1 and (a if jp == 0 else att):
                    mm(p_n[:, 0:H], nm[:, (jp - 1) % 2, :], ident16[:, :], start=True, stop=True)\
                        .then_inc(s_nmtp, 1)
                    return s_nmt, t * NJP + jp
                if g == 0 and b:
                    pe.wait_ge(s_xn1, t - 1)
                    transpose2(p_t, xn1).then_inc(s_x1Tp, 1)
                    return s_x1T, t - 1
                if g == 2 and b:
                    product(p_t[:, 0:NH], x1T, w_a).then_inc(s_hp, 1)
                    return s_hf, t - 1
                if g == 8 and a:
                    pe.wait_ge(s_o, t)
                    transpose2(p_t, o[:, :, :].rearrange("p h d -> p (h d)")).then_inc(s_oTp, 1)
                    return s_oT, t
                if g == 10 and a:
                    product(p_t, oT, w_o).then_inc(s_wo, 1)
                    return s_y0, t
                if g == 11 and b:
                    pe.wait_ge(s_hw, t - 1)
                    nc.tensor.transpose(p_n[0:NA, :], hw[:, :], ident[:, :]).then_inc(s_hTp, 1)
                    return s_hT, t - 1
                if g == 12 and b:
                    product(p_t, x1T, w_base, more=(hT[:, :], w_b[:, :])).then_inc(s_y2p, 1)
                    return s_y20, t - 1
                return None

            def wide(t, n, g, att, proj, a):
                jp, k = divmod(g, NI)
                if k and (a if jp == 0 else att):
                    pj = (jp - 1) % NJP
                    if k == 1:
                        pe.wait_ge(s_exp, t * NG + g - 1)
                        pe.wait_ge(s_vs[pj], batch_of(t - 1 if jp == 0 else t) * 16 + 16)
                        if jp == 0:
                            pe.wait_ge(s_part, t * NJP - 1)
                        else:
                            pe.wait_ge((s_xT, s_qkf, s_v)[jp - 1], n + 1)
                        pv(pj, 0)
                    elif k == 2:
                        pv(pj, 1).then_inc(s_pv, 1)
                    else:
                        transpose_parts(t * NJP + jp - 1)
                if k == 0 and jp and proj:
                    if att:
                        pe.wait_ge(s_part, t * NJP + jp - 1)
                    if jp == 1:
                        pe.wait_ge(s_xn, n + 1)
                        pe.wait_ge(s_v, n)
                        transpose2(pw[:, 0:2 * P], xn).then_inc(s_xTp, 1)
                    elif jp == 2:
                        pe.wait_ge(s_xT, n + 1)
                        for m, w in enumerate((w_q, w_k)):
                            for e in range(2):
                                last = product(pw[:, (2 * m + e) * P:(2 * m + e + 1) * P],
                                               w[:, :, e * P:(e + 1) * P], xT)
                        last.then_inc(s_qkp, 1)
                    else:
                        pe.wait_ge(s_qkf, n + 1)
                        product(pw[:, 0:D], xT, w_v).then_inc(s_vp, 1)

            def tile(t, n, att, proj, a, b):
                for g in range(NG):
                    jp, k = divmod(g, NI)
                    if att:
                        if k == 0:
                            pe.wait_ge(s_tw[jp], t * 16 + 16)
                            pe.wait_ge(s_ks[jp], batch_of(t) * 96 + 96)
                        if jp == 0:
                            pe.wait_ge(s_mask, t * NI + k + 1)
                        free = t * NG + g - DIST[g] + 1
                        if not (isinstance(free, int) and free <= 0):
                            pe.wait_ge(s_exp, free)
                        scores(g, 0)
                    read = mixed(t, g, att, a, b)
                    if att:
                        scores(g, 1).then_inc(s_scores, 1)
                    if read is not None:
                        pe.wait_ge(*read)
                    if (a if g == 0 else att):
                        transpose_max(t * NG + g)
                    wide(t, n, g, att, proj, a)
                    if (a if g == 0 else att):
                        shift((g - 1) % NG, t * NG + g)

            passes(pe, tile)

        @block.scalar
        def _(act):
            A = nc.scalar.activation
            act.wait_ge(s_const, N_CONST)
            act.wait_ge(s_cdve, 1)

            def copy(dst, src):
                return A(dst, src, ACT.Copy)

            def exp(g, count, free):
                jp, i = divmod(g, NI)
                act.wait_ge(s_shift, count)
                if not (isinstance(free, int) and free <= 0):
                    act.wait_ge(s_pv, free)
                A(prob[:, jp % 2, :, :, i * IW:(i + 1) * IW],
                  sc[:, 2 * RING[g]:2 * RING[g] + 2, :].rearrange("p c (h i) -> p c h i", i=IW),
                  ACT.Exp).then_inc(s_exp, 1)

            def tile(t, n, att, proj, a, b):
                for g in range(NG):
                    jp, k = divmod(g, NI)
                    stage = t * NJP + jp - 1
                    pj = (jp - 1) % NJP
                    old = a if jp == 0 else att
                    if k == 1 and old:
                        act.wait_ge(s_nmtp, stage + 1)
                        if jp == 1 and a:
                            act.wait_ge(s_dm, t)
                        copy(nmt[:, pj, :], p_n[:, 0:H]).then_inc(s_nmt, 1)
                    if g == 0 and b:
                        act.wait_ge(s_x1Tp, t - 1)
                        copy(x1T[:, :, :].rearrange("p c i -> p (c i)"), p_t).then_inc(s_x1T, 1)
                    if g == 2 and b:
                        act.wait_ge(s_hp, t - 1)
                        copy(hf[:, :], p_t[:, 0:NH]).then_inc(s_hf, 1)
                    if g == 8 and a:
                        act.wait_ge(s_oTp, t)
                        copy(oT[:, :, :].rearrange("p c i -> p (c i)"), p_t).then_inc(s_oT, 1)
                    if g == 10 and a:
                        act.wait_ge(s_wo, t)
                        copy(y0[:, :], p_t).then_inc(s_y0, 1)
                    if g == 11 and b:
                        act.wait_ge(s_hTp, t - 1)
                        copy(hT[:, :], p_n[0:NA, :]).then_inc(s_hT, 1)
                    if g == 12 and b:
                        act.wait_ge(s_y2p, t - 1)
                        copy(y20[:, :], p_t).then_inc(s_y20, 1)
                    if k == 2 and old:
                        act.wait_ge(s_pv, stage + 1)
                        copy(ot[:, :, :].rearrange("p c i -> p (c i)"), pw[:, :]).then_inc(s_ot, 1)
                    if k == 3 and old:
                        act.wait_ge(s_ott, stage + 1)
                        if jp == 1 and a:
                            act.wait_ge(s_wp, t)
                        copy(parts[:, pj, :, :],
                             pw[:, :].rearrange("p (h d) -> p h d", d=32)[:, :, 0:17]).then_inc(s_part, 1)
                    if g == 4 and proj:
                        act.wait_ge(s_xTp, n + 1)
                        copy(xT[:, :, :].rearrange("p c i -> p (c i)"), pw[:, 0:2 * P]).then_inc(s_xT, 1)
                    if g == 8 and proj:
                        act.wait_ge(s_qkp, n + 1)
                        act.wait_ge(s_qks, n)
                        for e in range(4):
                            last = A(qkf[:, e, :], pw[:, e * P:(e + 1) * P], ACT.Identity,
                                     bias=b_qk[:, e:e + 1])
                        last.then_inc(s_qkf, 1)
                    if g == 3 and b:
                        act.wait_ge(s_lg, t - 1)
                        A(eg[:, :], lg[:, :], ACT.Exp, bias=nlm[:, 0:1], accum_out=gsum[:, :]).then_inc(s_eg, 1)
                    if g == 5 and a:
                        act.wait_ge(s_dm, t)
                        A(wst[:, :, :], dm[:, :, :], ACT.Exp).then_inc(s_wst, 1)
                    if (a if g == 0 else att):
                        pg = (g - 1) % NG
                        exp(pg, t * NG + g, (t - 1 if g == 0 else t) * NJP + pg // NI - 1)

            passes(act, tile)

        @block.vector
        def _(dve):
            v = nc.vector
            dve.wait_ge(s_const, N_CONST)
            v.tensor_scalar(w_k[:, :, :], w_k[:, :, :], HD ** -0.5, None, ALU.mult)
            v.tensor_scalar(b_qk[:, 2:4], b_qk[:, 2:4], HD ** -0.5, None, ALU.mult).then_inc(s_cdve, 1)
            v.memset(tf[:, 0:1], 0.0)
            v.tensor_copy(tf[:, 1:1 + MAX_LEN], relf[:, NREL - MAX_LEN:NREL])
            v.tensor_copy(tf[:, 1 + MAX_LEN:1 + MAX_LEN + NREL], relf[:, :])
            v.tensor_copy(tf[:, 1 + MAX_LEN + NREL:NU + 1],
                          relf[:, NREL - 1:NREL].to_broadcast((HD, NU - MAX_LEN - NREL)))
            dve.drain()
            v.tensor_copy(th[:, :], tf[:, :]).then_inc(s_tsplit, 1)
            dve.drain()
            v.tensor_tensor(tl[:, :], tf[:, :], th[:, :], ALU.subtract).then_inc(s_tsplit, 1)
            dve.wait_ge(s_cpool, 1)

            def maxima(g, count):
                dve.wait_ge(s_scores, count)
                v.tensor_reduce(r1[:, :], sc[:, 2 * RING[g]:2 * RING[g] + 2, :]
                                .rearrange("p c (h i) -> p (c h) i", i=IW),
                                axis=AX.X, op=ALU.max, apply_transpose=True)
                dve.drain()
                v.tensor_tensor(r2[:, :], r1[:, 0:H], r1[:, H:2 * H], ALU.max).then_inc(s_rmax, 1)

            def spread(g, count):
                jp, i = divmod(g, NI)
                dve.wait_ge(s_maxT, count)
                part = nm[:, jp % 2, i * IW:(i + 1) * IW]
                v.tensor_reduce(part, p_max.rearrange("h (q i) -> h i q", i=IW), axis=AX.X, op=ALU.max,
                                negate=True)
                dve.drain()
                v.tensor_tensor(nmm[0:H, :, :], part.rearrange("h (a i) -> h a i", a=1)
                                .to_broadcast((H, H, IW)), mask_h[:, :, :], ALU.mult).then_inc(s_nm, 1)

            def stats(st, mv, src):
                v.bn_stats(st[:, :], src)
                dve.drain()
                return v.bn_aggr(mv[:, :], st[:, :])

            def normal(dst, src, mv, rs):
                return v.tensor_scalar(dst, src, mv[:, 0:1], rs[:, 0:1], ALU.subtract, ALU.mult)

            def side(g, t, n, proj, a, b):
                if g == 0 and proj:
                    dve.wait_ge(s_x, n * 16)
                    stats(st0, mv0, xin[:, :]).then_inc(s_mv0, 1)
                if g == 1 and proj:
                    dve.wait_ge(s_rs0, n + 1)
                    dve.wait_ge(s_xTp, n)
                    normal(xn[:, :], xin[:, :], mv0, rs0).then_inc(s_xn, 1)
                if g == 2 and b:
                    dve.wait_ge(s_hf, t - 1)
                    v.tensor_tensor(lg[:, :], hf[:, NA:NH], b_rt[:, :], ALU.add)
                    dve.drain()
                    v.tensor_reduce(nlm[:, :], lg[:, :], axis=AX.X, op=ALU.max, negate=True).then_inc(s_lg, 1)
                if g == 3 and b:
                    dve.wait_ge(s_eg, t - 1)
                    v.reciprocal(rg[:, :], gsum[:, :])
                    dve.drain()
                    v.tensor_scalar(gate[:, :], eg[:, :], rg[:, 0:1], None, ALU.mult)
                if g == 4 and a:
                    dve.wait_ge(s_nmt, t * NJP)
                    v.tensor_reduce(nmin[:, :], nmt[:, :, :].rearrange("p j h -> p h j"), axis=AX.X,
                                    op=ALU.min)
                    dve.drain()
                    v.tensor_tensor(dm[:, :, :], nmin[:, :].rearrange("p (a h) -> p a h", a=1)
                                    .to_broadcast((P, NJP, H)), nmt[:, :, :], ALU.subtract).then_inc(s_dm, 1)
                if g == 4 and b:
                    ge = gate[:, :].rearrange("p (e a) -> p e a", a=1).to_broadcast((P, E, E))
                    gf = gate[:, :].rearrange("p (a f) -> p a f", a=1).to_broadcast((P, E, E))
                    dve.drain()
                    v.tensor_tensor(ceq[:, :, :], gf, ge, ALU.is_equal)
                    v.tensor_tensor(cgt[:, :, :], gf, ge, ALU.is_gt)
                if g == 5 and b:
                    dve.drain()
                    v.tensor_tensor(ceqt[:, :, :], ceq[:, :, :], tri[:, :, :], ALU.mult)
                    dve.drain()
                    v.tensor_tensor(cadd[:, :, :], cgt[:, :, :], ceqt[:, :, :], ALU.add)
                if g == 6 and b:
                    dve.drain()
                    v.tensor_reduce(rank[:, :], cadd[:, :, :], axis=AX.X, op=ALU.add)
                    dve.drain()
                    v.scalar_tensor_tensor(out=sw[:, :], in0=rank[:, :], scalar=2.0, in1=gate[:, :],
                                           op0=ALU.is_lt, op1=ALU.mult)
                if g == 7 and a:
                    dve.wait_ge(s_wp, t)
                    v.tensor_reduce(osum[:, :, :].rearrange("p h d -> p (h d)"),
                                    wp[:, :, :, :].rearrange("p j h d -> p (h d) j"), axis=AX.X, op=ALU.add)
                    dve.drain()
                    v.reciprocal(rden[:, :], osum[:, :, 16])
                    dve.drain()
                    v.tensor_tensor(o[:, :, :], osum[:, :, 0:HD], rden[:, :].rearrange("p (h a) -> p h a", a=1)
                                    .to_broadcast((P, H, HD)), ALU.mult).then_inc(s_o, 1)
                if g == 8 and b:
                    dve.drain()
                    v.tensor_reduce(ssum[:, :], sw[:, :], axis=AX.X, op=ALU.add)
                    dve.drain()
                    v.tensor_scalar(ssume[:, :], ssum[:, :], 1e-6, None, ALU.add)
                if g == 9 and b:
                    dve.drain()
                    v.reciprocal(rss[:, :], ssume[:, :])
                    dve.drain()
                    v.tensor_scalar(swn[:, :], sw[:, :], rss[:, 0:1], None, ALU.mult)
                    v.tensor_copy(hw[:, 0:R], hf[:, 0:R])
                    dve.drain()
                    v.tensor_tensor(hw[:, R:NA].rearrange("p (e r) -> p e r", r=R),
                                    hf[:, R:NA].rearrange("p (e r) -> p e r", r=R),
                                    swn[:, :].rearrange("p (e a) -> p e a", a=1).to_broadcast((P, E, R)),
                                    ALU.mult).then_inc(s_hw, 1)
                if g == 10 and a:
                    dve.wait_ge(s_y0, t)
                    v.tensor_tensor(y[:, :], y0[:, :], b_o[:, :], ALU.add)
                    dve.drain()
                    stats(st1, mv1, y[:, :]).then_inc(s_mv1, 1)
                if g == 12 and a:
                    dve.wait_ge(s_rs1, t)
                    normal(yn[:, :], y[:, :], mv1, rs1)
                    dve.drain()
                    dve.wait_ge(s_xr, t * 16)
                    if b:
                        dve.wait_ge(s_x1b, t - 1)
                    v.tensor_tensor(x1[:, :], yn[:, :], xr[:, :], ALU.add).then_inc(s_x1, 1)
                if g == 12 and proj:
                    dve.wait_ge(s_vp, n + 1)
                    dve.wait_ge(s_vst, n * 16)
                    v.tensor_tensor(vpad[:, :, 0:HD], pw[:, 0:D].rearrange("p (h d) -> p h d", d=HD),
                                    b_v[:, :].rearrange("p (h d) -> p h d", d=HD), ALU.add).then_inc(s_v, 1)
                if g == 13 and b:
                    dve.wait_ge(s_y20, t - 1)
                    v.tensor_tensor(y2[:, :], y20[:, :], b_base[:, :], ALU.add)
                    dve.drain()
                    stats(st3, mv3, y2[:, :]).then_inc(s_mv3, 1)
                if g == 13 and a:
                    dve.drain()
                    stats(st2, mv2, x1[:, :]).then_inc(s_mv2, 1)
                if g == 15 and b:
                    dve.wait_ge(s_rs3, t - 1)
                    normal(y2n[:, :], y2[:, :], mv3, rs3)
                if g == 15 and a:
                    dve.wait_ge(s_rs2, t)
                    normal(xn1[:, :], x1[:, :], mv2, rs2).then_inc(s_xn1, 1)
                if g == 15 and b:
                    dve.drain()
                    dve.wait_ge(s_x1b, t - 1)
                    dve.wait_ge(s_out, (t - 1) * 16)
                    v.tensor_tensor(res[:, :], y2n[:, :], x1b[:, :], ALU.add).then_inc(s_res, 1)

            def tile(t, n, att, proj, a, b):
                for g in range(NG):
                    if (a if g == 0 else att):
                        spread((g - 1) % NG, t * NG + g)
                    if att:
                        maxima(g, t * NG + g + 1)
                    side(g, t, n, proj, a, b)

            passes(dve, tile)


def kernel(**inputs):
    import concourse.bacc as bacc
    from concourse.bass_utils import run_bass_kernel_spmd

    def a(name):
        return np.asarray(inputs[name])

    laid = {
        "x": a("L0_attn_x").reshape(B * L, D),
        "wqT": a("L0_attn_Wq").T, "bq": a("L0_attn_bq"),
        "wkT": a("L0_attn_Wk").T, "bk": a("L0_attn_bk"),
        "wvT": a("L0_attn_Wv").T, "bv": a("L0_attn_bv"),
        "woT": a("L0_attn_Wo").T, "bo": a("L0_attn_bo"),
        "relT": a("L0_attn_rel_emb").T,
        "baseT": a("L0_ffn_base_W").T, "base_b": a("L0_ffn_base_b"),
        "shAT": a("L0_ffn_shared_A").T, "shBT": a("L0_ffn_shared_B").T,
        "roAT": a("L0_ffn_routed_A").reshape(E * R, D).T,
        "roBT": a("L0_ffn_routed_B").transpose(0, 2, 1).reshape(E * R, D),
        "rtT": a("L0_ffn_router_W").T, "rtb": a("L0_ffn_router_b"),
    }
    nc = bacc.Bacc("TRN2", target_bir_lowering=False, num_devices=1)
    arrays, aps = {}, {}
    for name, array in laid.items():
        arrays[name] = np.ascontiguousarray(array)
        aps[name] = nc.dram_tensor(name, arrays[name].shape, mybir.dt.from_np(arrays[name].dtype),
                                   kind="ExternalInput").ap()
    out = nc.dram_tensor("out", (B * L, D), mybir.dt.float32, kind="ExternalOutput").ap()
    sandwich_kernel(nc, out=out, **aps)
    r = run_bass_kernel_spmd(nc, [arrays], core_ids=[0])
    return r.results[0]["out"].reshape(B, L, D)
```

```python
from contextlib import ExitStack

import numpy as np

import concourse.bass as bass
from concourse import mybir

B, L, D = 16, 1024, 256
H, HD = 16, 16
MAX_LEN = 512
NREL = 2 * MAX_LEN - 1
E, R = 6, 16
P = 128
NT = B * L // P
TPB = L // P
JC = L // P
NJP = JC // 2
IW = 32
NI = P // IW
NG = NJP * NI
ROWS = 96
SPLIT = (0, 0, 1)
SPLIT_ST = (0, 1, 0)
TWC = 3 * P
NU = 2 * L
NA = R + E * R
NH = NA + E
EPS = 1e-5
NBUF = 3


def buffer(t, g):
    return (t * NG + g) % NBUF


def sandwich_kernel(nc, x, wqT, bq, wkT, bk, wvT, bv, woT, bo, relT, baseT, base_b,
                    shAT, shBT, roAT, roBT, rtT, rtb, out):
    f32, f16 = mybir.dt.float32, mybir.dt.float16
    ALU = mybir.AluOpType
    ACT = mybir.ActivationFunctionType
    AX = mybir.AxisListType

    qk_s = nc.dram_tensor("qk_s", (2, 2, B + 1, D, L), f16, kind="Internal").ap()
    v_s = nc.dram_tensor("v_s", ((B + 1) * TPB, P, H * 32), f32, kind="Internal").ap()
    t_s = nc.dram_tensor("t_s", (2, HD, NU + 1), f16, kind="Internal").ap()
    tw_s = nc.dram_tensor("tw_s", (ROWS, NU), f16, kind="Internal").ap()

    ctx = ExitStack()
    with ctx:
        def sb(name, shape, dt=f32):
            return ctx.enter_context(nc.sbuf_tensor(name, shape, dt))

        def sem(name):
            return ctx.enter_context(nc.semaphore(name))

        ident = sb("ident", [P, P])
        ident16 = sb("ident16", [H, H], f16)
        ones16 = sb("ones16", [P, P], f16)
        mask_h = sb("mask_h", [H, H, IW], f16)
        mask_q = sb("mask_q", [ROWS, H, IW], f16)
        mask_r = sb("mask_r", [ROWS, H, IW], f16)
        tri = sb("tri", [P, E, E])
        mhalf = sb("mhalf", [P, 1])
        eps = sb("eps", [P, 1])
        one = sb("one", [P, 1])
        w_q = sb("w_q", [P, 2, D])
        w_k = sb("w_k", [P, 2, D])
        w_v = sb("w_v", [P, 2, D])
        w_o = sb("w_o", [P, 2, D])
        w_base = sb("w_base", [P, 2, D])
        w_a = sb("w_a", [P, 2, NH])
        w_b = sb("w_b", [NA, D])
        w_q2 = sb("w_q2", [P, 2, 2, D], f16)
        w_k2 = sb("w_k2", [P, 2, 2, D], f16)
        w_v2 = sb("w_v2", [P, 2, 2, D], f16)
        w_o2 = sb("w_o2", [P, 2, 2, D], f16)
        w_base2 = sb("w_base2", [P, 2, 2, D], f16)
        w_a2 = sb("w_a2", [P, 2, 2, NH], f16)
        w_b2 = sb("w_b2", [NA, 2, D], f16)
        b_qk = sb("b_qk", [P, 4])
        b_v = sb("b_v", [P, D])
        b_o = sb("b_o", [P, D])
        b_base = sb("b_base", [P, D])
        b_rt = sb("b_rt", [P, E])
        relf = sb("relf", [HD, NREL])
        tf = sb("tf", [HD, NU + 1])
        th = sb("th", [HD, NU + 1], f16)
        tl = sb("tl", [HD, NU + 1], f16)
        tw = sb("tw", [ROWS, NJP, TWC], f16)
        ks = sb("ks", [ROWS, H // 2, L], f16)
        vs = sb("vs", [P, JC, H, 32])
        raw = sb("raw", [ROWS, H, P], f16)
        qm = sb("qm", [ROWS, NI, H, IW], f16)
        rm = sb("rm", [ROWS, NI, IW // 2, H, 2], f16)
        prob = sb("prob", [P, 2, 2, H, P])
        r1 = sb("r1", [P, 2 * H])
        r2 = sb("r2", [P, H])
        nm = sb("nm", [H, 2, P], f16)
        nmm = sb("nmm", [P, H, IW], f16)
        ot = sb("ot", [P, 4, P])
        parts = sb("parts", [P, NJP, H, 17])
        nmt = sb("nmt", [P, NJP, H])
        nmin = sb("nmin", [P, H])
        dm = sb("dm", [P, NJP, H])
        wst = sb("wst", [P, NJP, H])
        wp = sb("wp", [P, NJP, H, 17])
        osum = sb("osum", [P, H, 17])
        rden = sb("rden", [P, H])
        o = sb("o", [P, H, HD])
        oT = sb("oT", [P, 2, P])
        oT2 = sb("oT2", [P, 2, 2, P], f16)
        xin = sb("xin", [P, D])
        xn = sb("xn", [P, D])
        xT = sb("xT", [P, 2, P])
        xT2 = sb("xT2", [P, 2, 2, P], f16)
        st0 = sb("st0", [P, 6])
        mv0 = sb("mv0", [P, 2])
        ve0 = sb("ve0", [P, 1])
        rs0 = sb("rs0", [P, 1])
        qkf = sb("qkf", [P, 4, P])
        qkb = sb("qkb", [P, 4, P])
        qkh = sb("qkh", [P, 4, P], f16)
        qkl = sb("qkl", [P, 4, P], f16)
        vf = sb("vf", [P, D])
        vpad = sb("vpad", [P, H, 32])
        xr = sb("xr", [P, D])
        y0 = sb("y0", [P, D])
        y = sb("y", [P, D])
        yn = sb("yn", [P, D])
        x1 = sb("x1", [P, D])
        x1b = sb("x1b", [P, D])
        xn1 = sb("xn1", [P, D])
        x1T = sb("x1T", [P, 2, P])
        x1T2 = sb("x1T2", [P, 2, 2, P], f16)
        st1 = sb("st1", [P, 6])
        mv1 = sb("mv1", [P, 2])
        ve1 = sb("ve1", [P, 1])
        rs1 = sb("rs1", [P, 1])
        st2 = sb("st2", [P, 6])
        mv2 = sb("mv2", [P, 2])
        ve2 = sb("ve2", [P, 1])
        rs2 = sb("rs2", [P, 1])
        st3 = sb("st3", [P, 6])
        mv3 = sb("mv3", [P, 2])
        ve3 = sb("ve3", [P, 1])
        rs3 = sb("rs3", [P, 1])
        hf = sb("hf", [P, NH])
        lg = sb("lg", [P, E])
        nlm = sb("nlm", [P, 1])
        eg = sb("eg", [P, E])
        gsum = sb("gsum", [P, 1])
        rg = sb("rg", [P, 1])
        gate = sb("gate", [P, E])
        cgt = sb("cgt", [P, E, E])
        ceq = sb("ceq", [P, E, E])
        ceqt = sb("ceqt", [P, E, E])
        cadd = sb("cadd", [P, E, E])
        rank = sb("rank", [P, E])
        sw = sb("sw", [P, E])
        ssum = sb("ssum", [P, 1])
        ssume = sb("ssume", [P, 1])
        rss = sb("rss", [P, 1])
        swn = sb("swn", [P, E])
        hw = sb("hw", [P, NA])
        hT = sb("hT", [NA, P])
        hT2 = sb("hT2", [NA, 2, P], f16)
        osum2 = sb("osum2", [P, 2, H, 17])
        y20 = sb("y20", [P, D])
        y2 = sb("y2", [P, D])
        y2n = sb("y2n", [P, D])
        res = sb("res", [P, D])

        sc = ctx.enter_context(nc.psum_tensor("sc", [P, 6, 512], f32))
        pw = ctx.enter_context(nc.psum_tensor("pw", [P, 512], f32))
        pm = ctx.enter_context(nc.psum_tensor("pm", [P, 512], f32))
        p_max = pm[0:H, 0:P]
        p_n = pm[:, P:2 * P]
        p_t = pm[:, 2 * P:4 * P]

        s_const = sem("s_const")
        s_cpool = sem("s_cpool")
        s_cdve = sem("s_cdve")
        s_tsplit = sem("s_tsplit")
        s_tst = sem("s_tst")
        s_tws = sem("s_tws")
        s_tw = [sem(f"s_tw{j}") for j in range(NJP)]
        s_ks = [sem(f"s_ks{j}") for j in range(NJP)]
        s_vs = [sem(f"s_vs{j}") for j in range(NJP)]
        s_raw = sem("s_raw")
        s_mask = sem("s_mask")
        s_scores = sem("s_scores")
        s_rmax = sem("s_rmax")
        s_maxT = sem("s_maxT")
        s_nm = sem("s_nm")
        s_shift = sem("s_shift")
        s_exp = sem("s_exp")
        s_pv = sem("s_pv")
        s_ot = sem("s_ot")
        s_ott = sem("s_ott")
        s_part = sem("s_part")
        s_dm = sem("s_dm")
        s_wst = sem("s_wst")
        s_wp = sem("s_wp")
        s_osum = sem("s_osum")
        s_o = sem("s_o")
        s_oTp = sem("s_oTp")
        s_oT = sem("s_oT")
        s_wo = sem("s_wo")
        s_y0 = sem("s_y0")
        s_nmtp = sem("s_nmtp")
        s_nmt = sem("s_nmt")
        s_mv1 = sem("s_mv1")
        s_rs1 = sem("s_rs1")
        s_xr = sem("s_xr")
        s_x1 = sem("s_x1")
        s_mv2 = sem("s_mv2")
        s_rs2 = sem("s_rs2")
        s_xn1 = sem("s_xn1")
        s_x1Tp = sem("s_x1Tp")
        s_x1T = sem("s_x1T")
        s_x1b = sem("s_x1b")
        s_hp = sem("s_hp")
        s_hf = sem("s_hf")
        s_lg = sem("s_lg")
        s_eg = sem("s_eg")
        s_hw = sem("s_hw")
        s_hTp = sem("s_hTp")
        s_hT = sem("s_hT")
        s_y2p = sem("s_y2p")
        s_y20 = sem("s_y20")
        s_mv3 = sem("s_mv3")
        s_rs3 = sem("s_rs3")
        s_res = sem("s_res")
        s_out = sem("s_out")
        s_x = sem("s_x")
        s_mv0 = sem("s_mv0")
        s_rs0 = sem("s_rs0")
        s_xn = sem("s_xn")
        s_xTp = sem("s_xTp")
        s_xT = sem("s_xT")
        s_qkp = sem("s_qkp")
        s_qkf = sem("s_qkf")
        s_qks = sem("s_qks")
        s_qkst = sem("s_qkst")
        s_vp = sem("s_vp")
        s_vf = sem("s_vf")
        s_v = sem("s_v")
        s_vst = sem("s_vst")
        s_nmr = sem("s_nmr")
        s_oT2 = sem("s_oT2")
        s_xT2 = sem("s_xT2")
        s_x1T2 = sem("s_x1T2")
        s_hT2 = sem("s_hT2")
        s_y = sem("s_y")
        s_yn = sem("s_yn")
        s_y2 = sem("s_y2")
        s_y2n = sem("s_y2n")
        s_step = sem("s_step")

        N_CONST = 20 * 16
        block = ctx.enter_context(nc.Block())

        def batch_of(t):
            return t // TPB

        assert (NT - 2) % NBUF == 0

        def passes(eng, tile):
            tile(-TPB, 0, att=False, proj=True, a=False, b=False)
            with eng.Fori(1, TPB) as n:
                tile(n - TPB, n, att=False, proj=True, a=False, b=False)
            tile(0, TPB, att=True, proj=True, a=False, b=False, ph=0)
            tile(1, TPB + 1, att=True, proj=True, a=True, b=False, ph=1)
            with nc.Fori(2, NT, NBUF, engines=(eng.engine,), hint_back_edge=True) as t:
                for k in range(NBUF):
                    tile(t + k, t + (k + TPB), att=True, proj=True, a=True, b=True, ph=(2 + k) % NBUF)
            tile(NT, None, att=False, proj=False, a=True, b=True, ph=NT % NBUF)
            tile(NT + 1, None, att=False, proj=False, a=False, b=True)

        @block.sync
        def _(sp):
            def const(dst, src):
                sp.dma_start(dst, src).then_inc(s_const, 16)

            def two(a):
                return a.rearrange("(c p) n -> p c n", p=P)

            sp.sem_inc(s_out, 16)
            const(relf[:, :], relT)
            for dst, src in ((w_q, wqT), (w_k, wkT), (w_v, wvT), (w_o, woT), (w_base, baseT)):
                const(dst[:, :, :], two(src))
            const(w_a[:, :, 0:R], two(shAT))
            const(w_a[:, :, R:NA], two(roAT))
            const(w_a[:, :, NA:NH], two(rtT))
            const(w_b[0:R, :], shBT)
            const(w_b[R:NA, :], roBT)
            for c in range(2):
                const(b_qk[:, c:c + 1], bq[c * P:(c + 1) * P].rearrange("(p a) -> p a", a=1))
                const(b_qk[:, 2 + c:3 + c], bk[c * P:(c + 1) * P].rearrange("(p a) -> p a", a=1))
            for dst, src in ((b_v, bv), (b_o, bo), (b_base, base_b), (b_rt, rtb)):
                const(dst[:, :], src.rearrange("(a n) -> a n", a=1).to_broadcast((P, src.shape[0])))
            const(xin[:, :], x[0:P, :])
            assert N_CONST == 16 * 20

            sp.wait_ge(s_xn, 1)
            sp.dma_start(xin[:, :], x[P:2 * P, :]).then_inc(s_x, 16)

            sp.wait_ge(s_tsplit, 2)
            sp.dma_start(t_s[0], th[:, :]).then_inc(s_tst, 16)
            sp.dma_start(t_s[1], tl[:, :]).then_inc(s_tst, 16)
            sp.wait_ge(s_tst, 32)
            for s in range(2):
                for k, part in enumerate(SPLIT_ST):
                    r = (3 * s + k) * HD
                    sp.dma_start(tw_s[r:r + HD, :], t_s[part, :, 1 - s:1 - s + NU]).then_inc(s_tws, 16)
            sp.wait_ge(s_tws, 6 * 16)

            def load_window(it, jp):
                u = (TPB - 1) * P - it * P + 2 * P * jp
                sp.dma_start(tw[:, jp, :], tw_s[:, bass.ds(u, TWC)] if not isinstance(u, int)
                             else tw_s[:, u:u + TWC]).then_inc(s_tw[jp], 16)

            def load_raw(b, it):
                for s in range(2):
                    for k, part in enumerate(SPLIT):
                        r = (3 * s + k) * HD
                        src = qk_s[part, 0, b].rearrange("(h d) t -> d h t", d=HD)
                        sp.dma_start(raw[r:r + HD, :, :], src[:, :, it * P:it * P + P] if isinstance(it, int)
                                     else src[:, :, bass.ds(it * P, P)]).then_inc(s_raw, 16)

            def load_keys(b, jp):
                for s in range(2):
                    for k, part in enumerate(SPLIT_ST):
                        r = (3 * s + k) * HD
                        src = qk_s[part, 1, b].rearrange("(h s d) t -> s d h t", s=2, d=HD)
                        j = 2 * P * jp
                        sp.dma_start(ks[r:r + HD, :, j:j + 2 * P], src[s, :, :, j:j + 2 * P])\
                          .then_inc(s_ks[jp], 16)

            def load_values(b, jp):
                n = b * TPB + 2 * jp
                src = v_s[n:n + 2] if isinstance(n, int) else v_s[bass.ds(n, 2)]
                sp.dma_start(vs[:, 2 * jp:2 * jp + 2, :, :].rearrange("p c h d -> p c (h d)"),
                             src.rearrange("c p f -> p c f")).then_inc(s_vs[jp], 16)

            def after(sem, value):
                sp.wait_ge(sem, value)
                sp.sem_inc(s_step, 1)

            def tile(b, it, att, proj, a, bb, new=False, last=False, end=False, wrap=False, first=False):
                t = b * TPB + it
                n = t + TPB
                if att:
                    if not first:
                        after(s_scores, t * NG)
                        load_window(it, NJP - 1)
                        if new:
                            after(s_qkst, n * 64)
                            load_keys(b, NJP - 1)
                    after(s_mask, t * NI + NI)
                    if last:
                        load_raw(b + 1, 0)
                    else:
                        load_raw(b, it + 1)
                if a:
                    after(s_x1, t - 1)
                    row = (t - 1) * P
                    sp.dma_start(xr[:, :], x[row:row + P, :] if isinstance(row, int)
                                 else x[bass.ds(row, P), :]).then_inc(s_xr, 16)
                if new:
                    after(s_pv, t * NJP)
                    after(s_vst, n * 16)
                    load_values(b, NJP - 1)
                if att and not end:
                    nit = 0 if last else it + 1
                    after(s_scores, t * NG + NI)
                    load_window(nit, 0)
                    if last:
                        load_keys(b + 1, 0)
                if proj:
                    after(s_xn, n + 2)
                    row = it * P if wrap else (n + 2) * P
                    sp.dma_start(xin[:, :], x[row:row + P, :] if isinstance(row, int)
                                 else x[bass.ds(row, P), :]).then_inc(s_x, 16)
                if last and not end:
                    after(s_pv, t * NJP + 1)
                    load_values(b + 1, 0)
                if att and not end:
                    after(s_scores, t * NG + 2 * NI)
                    load_window(nit, 1)
                    if last:
                        load_keys(b + 1, 1)
                if proj:
                    after(s_qks, n + 1)
                    for part, src in ((0, qkh), (1, qkl)):
                        for sel in range(2):
                            dst = qk_s[part, sel, b + 1].rearrange("(c p) t -> p c t", p=P)
                            sp.dma_start(dst[:, :, it * P:it * P + P] if isinstance(it, int)
                                         else dst[:, :, bass.ds(it * P, P)],
                                         src[:, 2 * sel:2 * sel + 2, :]).then_inc(s_qkst, 16)
                if last and not end:
                    after(s_pv, t * NJP + 2)
                    load_values(b + 1, 1)
                if att and not end:
                    after(s_scores, t * NG + 3 * NI)
                    load_window(nit, 2)
                    if last:
                        load_keys(b + 1, 2)
                if proj:
                    after(s_v, n + 1)
                    dst = v_s[n] if isinstance(n, int) else v_s[bass.ds(n, 1)].rearrange("a p f -> (a p) f")
                    sp.dma_start(dst, vpad[:, :, :].rearrange("p h d -> p (h d)")).then_inc(s_vst, 16)
                if last and not end:
                    after(s_pv, t * NJP + 3)
                    load_values(b + 1, 2)
                if bb:
                    after(s_res, t - 1)
                    row = (t - 2) * P
                    sp.dma_start(out[row:row + P, :] if isinstance(row, int)
                                 else out[bass.ds(row, P), :], res[:, :]).then_inc(s_out, 16)

            tile(-1, 0, False, True, False, False)
            with sp.Fori(1, TPB) as it:
                tile(-1, it, False, True, False, False)
            for jp in range(NJP):
                load_window(0, jp)
            sp.wait_ge(s_qkst, TPB * 64)
            load_raw(0, 0)
            load_keys(0, 0)
            sp.wait_ge(s_vst, TPB * 16)
            load_values(0, 0)
            for jp in range(1, NJP):
                load_keys(0, jp)
                load_values(0, jp)
            tile(0, 0, True, True, False, False, first=True)
            tile(0, 1, True, True, True, False)
            with sp.Fori(2, TPB - 1) as it:
                tile(0, it, True, True, True, True)
            tile(0, TPB - 1, True, True, True, True, last=True)

            def batch(b, wrap=False, turn=False, end=False):
                tile(b, 0, True, True, True, True, new=True, wrap=wrap)
                with sp.Fori(1, TPB - 1 - turn) as it:
                    tile(b, it, True, True, True, True, wrap=wrap)
                if turn:
                    tile(b, TPB - 2, True, True, True, True, wrap=True)
                tile(b, TPB - 1, True, True, True, True, last=True, end=end, wrap=wrap or turn)

            with sp.Fori(1, B - 2) as b:
                batch(b)
            batch(B - 2, turn=True)
            batch(B - 1, wrap=True, end=True)
            tile(B, 0, False, False, True, True)
            tile(B, 1, False, False, False, True)
            sp.wait_ge(s_out, NT * 16 + 16)
            sp.wait_ge(s_x, (NT + TPB + 1) * 16)
            sp.wait_ge(s_qkst, (NT + TPB) * 64)
            sp.wait_ge(s_vst, (NT + TPB) * 16)

        @block.gpsimd
        def _(pool):
            g = nc.gpsimd
            g.memset(ident[:, :], 1.0)
            g.memset(ident16[:, :], 1.0)
            g.memset(ones16[:, :], 1.0)
            g.memset(mask_h[:, :, :], 1.0)
            g.memset(mask_q[:, :, :], 1.0)
            g.memset(mask_r[:, :, :], 1.0)
            g.memset(tri[:, :, :], 1.0)
            g.memset(mhalf[:, :], -0.5)
            g.memset(eps[:, :], EPS)
            g.memset(one[:, :], 1.0)
            g.memset(vpad[:, :, :], 1.0)
            g.memset(nmm[:, :, :], 0.0)
            pool.drain()

            def keep(v, op, base, pattern, mult):
                g.affine_select(out=v, in_=v, compare_op=op, fill=0.0, base=base, pattern=pattern,
                                channel_multiplier=mult)

            keep(ident[:, :], ALU.is_equal, 0, [[-1, P]], 1)
            keep(ident16[:, :], ALU.is_equal, 0, [[-1, H]], 1)
            keep(ones16[:, :], ALU.is_ge, H - 1, [[0, P]], -1)
            keep(mask_h[:, :, :], ALU.is_equal, 0, [[-1, H], [0, IW]], 1)
            half = ROWS // 2
            q4 = mask_q[:, :, :].rearrange("p (h s) i -> p h s i", s=2)
            r4 = mask_r[:, :, :].rearrange("p h (i s) -> p h i s", s=2)
            keep(q4[:, :, 0, :], ALU.is_ge, half - 1, [[0, H // 2], [0, IW]], -1)
            keep(q4[:, :, 1, :], ALU.is_ge, -half, [[0, H // 2], [0, IW]], 1)
            keep(r4[:, :, :, 0], ALU.is_ge, half - 1, [[0, H], [0, IW // 2]], -1)
            keep(r4[:, :, :, 1], ALU.is_ge, -half, [[0, H], [0, IW // 2]], 1)
            keep(tri[:, :, :], ALU.is_gt, 0, [[1, E], [-1, E]], 0)
            pool.drain().then_inc(s_cpool, 1)

            def mask(i):
                src = raw[:, :, i * IW:(i + 1) * IW]
                g.tensor_tensor(qm[:, i, :, :], src, mask_q[:, :, :], ALU.mult)
                g.tensor_tensor(rm[:, i, :, :, :].rearrange("p i h s -> p h i s"),
                                src.rearrange("p h (i s) -> p h i s", s=2),
                                mask_r[:, :, :].rearrange("p h (i s) -> p h i s", s=2),
                                ALU.mult).then_inc(s_mask, 1)

            def rstd(dst, mv, ve):
                g.tensor_tensor(ve[:, :], mv[:, 1:2], eps[:, :], ALU.add)
                pool.drain()
                return g.tensor_tensor(dst[:, :], ve[:, :], mhalf[:, :], ALU.pow)

            def split(two, whole, inc):
                g.tensor_tensor(two[0], whole, ones_like(whole), ALU.mult)
                pool.drain()
                g.tensor_tensor(two[1], whole, two[0], ALU.subtract).then_inc(inc, 1)

            def ones_like(x):
                return one[0:x.shape[0], :].to_broadcast(tuple(x.shape))

            def flat(x):
                return x.rearrange("p c i -> p (c i)")

            def tile(t, n, att, proj, a, b, ph=None):
                if att:
                    if isinstance(t, int) and t == 0:
                        pool.wait_ge(s_raw, 96)
                        for i in range(NI - 1):
                            mask(i)
                    pool.wait_ge(s_scores, t * NG)
                    mask(NI - 1)
                if b:
                    pool.wait_ge(s_x1T, t - 1)
                    split([flat(x1T2[:, k, :, :]) for k in range(2)], flat(x1T[:, :, :]), s_x1T2)
                    g.tensor_copy(x1b[:, :], x1[:, :])
                if proj:
                    pool.wait_ge(s_xT, n + 1)
                    split([flat(xT2[:, k, :, :]) for k in range(2)], flat(xT[:, :, :]), s_xT2)
                    pool.wait_ge(s_mv0, n + 2)
                    rstd(rs0, mv0, ve0).then_inc(s_rs0, 1)
                if a:
                    pool.wait_ge(s_wst, t)
                    pool.wait_ge(s_part, t * NJP)
                    g.tensor_tensor(wp[:, :, :, :].rearrange("p j h d -> p (j h) d"),
                                    parts[:, :, :, :].rearrange("p j h d -> p (j h) d"),
                                    wst[:, :, :].rearrange("p j (h a) -> p (j h) a", a=1)
                                    .to_broadcast((P, NJP * H, 17)), ALU.mult).then_inc(s_wp, 1)
                    pool.drain()
                    wf = wp[:, :, :, :].rearrange("p j h d -> p (j h d)")
                    o2 = osum2[:, :, :, :].rearrange("p j h d -> p (j h d)")
                    n2 = 2 * H * 17
                    g.tensor_tensor(o2, wf[:, 0:n2], wf[:, n2:2 * n2], ALU.add)
                    pool.drain()
                    g.tensor_tensor(osum[:, :, :].rearrange("p h d -> p (h d)"), o2[:, 0:n2 // 2],
                                    o2[:, n2 // 2:n2], ALU.add).then_inc(s_osum, 1)
                if proj:
                    pool.wait_ge(s_qkf, n + 1)
                    g.tensor_tensor(qkb[:, :, :], qkf[:, :, :],
                                    b_qk[:, :].rearrange("p (e a) -> p e a", a=1).to_broadcast((P, 4, P)), ALU.add)
                    pool.drain()
                    pool.wait_ge(s_qkst, n * 64)
                    split([flat(qkh[:, :, :]), flat(qkl[:, :, :])], flat(qkb[:, :, :]), s_qks)
                if a:
                    pool.wait_ge(s_oT, t)
                    split([flat(oT2[:, k, :, :]) for k in range(2)], flat(oT[:, :, :]), s_oT2)
                if proj:
                    pool.wait_ge(s_vst, n * 16)
                    pool.wait_ge(s_vf, n + 1)
                    g.tensor_tensor(vpad[:, :, 0:HD], vf[:, :].rearrange("p (h d) -> p h d", d=HD),
                                    b_v[:, :].rearrange("p (h d) -> p h d", d=HD), ALU.add).then_inc(s_v, 1)
                if b:
                    pool.wait_ge(s_hT, t - 1)
                    split([hT2[:, 0, :], hT2[:, 1, :]], hT[:, :], s_hT2)
                if a:
                    pool.wait_ge(s_y0, t)
                    g.tensor_tensor(y[:, :], y0[:, :], b_o[:, :], ALU.add).then_inc(s_y, 1)
                if b:
                    pool.wait_ge(s_y20, t - 1)
                    g.tensor_tensor(y2[:, :], y20[:, :], b_base[:, :], ALU.add).then_inc(s_y2, 1)
                if a:
                    pool.wait_ge(s_mv1, t)
                    rstd(rs1, mv1, ve1).then_inc(s_rs1, 1)
                if b:
                    pool.wait_ge(s_mv3, t - 1)
                    rstd(rs3, mv3, ve3).then_inc(s_rs3, 1)
                if a:
                    pool.wait_ge(s_xr, t * 16)
                    pool.wait_ge(s_yn, t)
                    g.tensor_tensor(x1[:, :], yn[:, :], xr[:, :], ALU.add).then_inc(s_x1, 1)
                if att:
                    pool.wait_ge(s_raw, t * 96 + 192)
                    pool.wait_ge(s_scores, t * NG + NG - NI + 1)
                    mask(0)
                if a:
                    pool.wait_ge(s_mv2, t)
                    rstd(rs2, mv2, ve2).then_inc(s_rs2, 1)
                if att:
                    for i in range(1, NI - 1):
                        pool.wait_ge(s_scores, t * NG + NG - NI + i + 1)
                        mask(i)
                if b:
                    pool.wait_ge(s_y2n, t - 1)
                    pool.wait_ge(s_out, (t - 1) * 16)
                    g.tensor_tensor(res[:, :], y2n[:, :], x1b[:, :], ALU.add).then_inc(s_res, 1)

            pool.wait_ge(s_mv0, 1)
            rstd(rs0, mv0, ve0).then_inc(s_rs0, 1)
            passes(pool, tile)

        @block.tensor
        def _(pe):
            mm = nc.tensor.matmul
            pe.wait_ge(s_const, N_CONST)
            pe.wait_ge(s_cpool, 1)
            pe.wait_ge(s_cdve, 1)

            def scores(g, c, buf):
                jp, i = divmod(g, NI)
                bank = sc[:, 2 * buf + c, :]
                out3 = bank.rearrange("p (h i) -> p h i", i=IW)
                j = (2 * jp + c) * P
                for h in range(H // 2):
                    last = mm(bank[:, 2 * h * IW:(2 * h + 2) * IW], ks[:, h, j:j + P],
                              qm[:, i, 2 * h:2 * h + 2, :].rearrange("p h i -> p (h i)"),
                              start=(h == 0), stop=False, skip_group_check=True)
                for k in range(IW // 2):
                    u = P - 1 - (i * IW + 2 * k) + c * P
                    last = mm(out3[:, :, 2 * k:2 * k + 2], tw[:, jp, u:u + P], rm[:, i, k, :, :],
                              start=False, stop=False, skip_group_check=True)
                return last

            def transpose_max(g_count):
                pe.wait_ge(s_rmax, g_count)
                nc.tensor.transpose(p_max, r2[:, :], ident[:, :]).then_inc(s_maxT, 1)

            def shift(buf, g_count):
                pe.wait_ge(s_nm, g_count)
                for c in range(2):
                    last = mm(sc[:, 2 * buf + c, :], ones16[:, :],
                              nmm[:, :, :].rearrange("p h i -> p (h i)"),
                              start=False, stop=True, skip_group_check=True)
                last.then_inc(s_shift, 1)

            def pv(jp, half):
                for col in (2 * half, 2 * half + 1):
                    for c in range(2):
                        for q in range(4):
                            h = 4 * col + q
                            last = mm(pw[32 * q:32 * q + 32, col * P:(col + 1) * P], vs[:, 2 * jp + c, h, :],
                                      prob[:, jp % 2, c, h, :], start=(c == 0), stop=(c == 1))
                return last

            def transpose_parts(stage):
                pe.wait_ge(s_ot, stage + 1)
                for col in range(4):
                    last = nc.tensor.transpose(pw[:, col * P:(col + 1) * P], ot[:, col, :], ident[:, :])
                last.then_inc(s_ott, 1)

            def transpose2(dst, src):
                for c in range(2):
                    last = nc.tensor.transpose(dst[:, c * P:(c + 1) * P], src[:, c * P:(c + 1) * P],
                                               ident[:, :])
                return last

            def product(dst, *pairs):
                steps = [(lhs(i), rhs(j)) for lhs, rhs in pairs for i, j in ((0, 0), (0, 1), (1, 0))]
                for m, (lhs, rhs) in enumerate(steps):
                    last = mm(dst, lhs, rhs, start=(m == 0), stop=(m == len(steps) - 1))
                return last

            def both(lhs, rhs, cols=slice(None)):
                return [(lambda i, c=c: lhs[:, i, c, cols], lambda j, c=c: rhs[:, j, c, :]) for c in range(2)]

            def mixed(t, g, att, a, b):
                jp, k = divmod(g, NI)
                if k == 1 and (a if jp == 0 else att):
                    mm(p_n[:, 0:H], nm[:, (jp - 1) % 2, :], ident16[:, :], start=True, stop=True)\
                        .then_inc(s_nmtp, 1)
                    return s_nmt, t * NJP + jp
                if g == 0 and b:
                    pe.wait_ge(s_xn1, t - 1)
                    transpose2(p_t, xn1).then_inc(s_x1Tp, 1)
                    return s_x1T, t - 1
                if g == 3 and b:
                    pe.wait_ge(s_x1T2, t - 1)
                    product(p_t[:, 0:NH], *both(x1T2, w_a2)).then_inc(s_hp, 1)
                    return s_hf, t - 1
                if g == 8 and a:
                    pe.wait_ge(s_o, t)
                    transpose2(p_t, o[:, :, :].rearrange("p h d -> p (h d)")).then_inc(s_oTp, 1)
                    return s_oT, t
                if g == 11 and a:
                    pe.wait_ge(s_oT2, t)
                    product(p_t, *both(oT2, w_o2)).then_inc(s_wo, 1)
                    return s_y0, t
                if g == 10 and b:
                    pe.wait_ge(s_hw, t - 1)
                    nc.tensor.transpose(p_n[0:NA, :], hw[:, :], ident[:, :]).then_inc(s_hTp, 1)
                    return s_hT, t - 1
                if g == 12 and b:
                    pe.wait_ge(s_hT2, t - 1)
                    product(p_t, *both(x1T2, w_base2), (lambda i: hT2[:, i, :], lambda j: w_b2[:, j, :]))\
                        .then_inc(s_y2p, 1)
                    return s_y20, t - 1
                return None

            def wide(t, n, g, att, proj, a):
                jp, k = divmod(g, NI)
                if k and (a if jp == 0 else att):
                    pj = (jp - 1) % NJP
                    if k == 1:
                        pe.wait_ge(s_exp, t * NG + g - 1)
                        pe.wait_ge(s_vs[pj], batch_of(t - 1 if jp == 0 else t) * 16 + 16)
                        if proj and jp < 3:
                            pe.wait_ge((s_xT, s_qkf, s_vf)[jp], n + 1)
                        else:
                            pe.wait_ge(s_part, t * NJP + jp - 1)
                        pv(pj, 0)
                    elif k == 2:
                        pv(pj, 1).then_inc(s_pv, 1)
                    else:
                        transpose_parts(t * NJP + jp - 1)
                if k == 0 and jp < 3 and proj:
                    if a if jp == 0 else att:
                        pe.wait_ge(s_part, t * NJP + jp - 1)
                    elif jp == 0:
                        pe.wait_ge(s_vf, n)
                    if jp == 0:
                        pe.wait_ge(s_xn, n + 1)
                        transpose2(pw[:, 0:2 * P], xn).then_inc(s_xTp, 1)
                    elif jp == 1:
                        pe.wait_ge(s_xT2, n + 1)
                        for m, w in enumerate((w_q2, w_k2)):
                            for e in range(2):
                                last = product(pw[:, (2 * m + e) * P:(2 * m + e + 1) * P],
                                               *both(w, xT2, slice(e * P, (e + 1) * P)))
                        last.then_inc(s_qkp, 1)
                    else:
                        pe.wait_ge(s_qkf, n + 1)
                        product(pw[:, 0:D], *both(xT2, w_v2)).then_inc(s_vp, 1)

            def tile(t, n, att, proj, a, b, ph=None):
                read = None
                for g in range(NG):
                    jp, k = divmod(g, NI)
                    old = a if g == 0 else att
                    if att:
                        if k == 0:
                            pe.wait_ge(s_tw[jp], t * 16 + 16)
                            pe.wait_ge(s_ks[jp], batch_of(t) * 96 + 96)
                        if jp == 0:
                            pe.wait_ge(s_mask, t * NI + k + 1)
                        free = t * NG + g - NBUF + 1
                        if not (isinstance(free, int) and free <= 0):
                            pe.wait_ge(s_exp, free)
                        scores(g, 0, buffer(ph, g))
                    if read is not None:
                        pe.wait_ge(*read)
                    if old:
                        transpose_max(t * NG + g)
                    if att:
                        scores(g, 1, buffer(ph, g)).then_inc(s_scores, 1)
                    wide_first = k == 1 or g in (0, 8)
                    if wide_first:
                        wide(t, n, g, att, proj, a)
                    if old:
                        pe.wait_ge(s_nmr, t * NG + g)
                    read = mixed(t, g, att, a, b)
                    if not wide_first:
                        wide(t, n, g, att, proj, a)
                    if old:
                        shift(buffer(ph, g - 1), t * NG + g)

            passes(pe, tile)

        @block.scalar
        def _(act):
            A = nc.scalar.activation
            act.wait_ge(s_const, N_CONST)
            act.wait_ge(s_cdve, 1)

            def copy(dst, src):
                return A(dst, src, ACT.Copy)

            def exp(g, buf, count, free):
                jp, i = divmod(g, NI)
                act.wait_ge(s_shift, count)
                if not (isinstance(free, int) and free <= 0):
                    act.wait_ge(s_pv, free)
                A(prob[:, jp % 2, :, :, i * IW:(i + 1) * IW],
                  sc[:, 2 * buf:2 * buf + 2, :].rearrange("p c (h i) -> p c h i", i=IW),
                  ACT.Exp).then_inc(s_exp, 1)

            def before(g, t, ph):
                pg = (g - 1) % NG
                exp(pg, buffer(ph, g - 1), t * NG + g, (t - 1 if g == 0 else t) * NJP + pg // NI - 1)

            def tile(t, n, att, proj, a, b, ph=None):
                for g in range(NG):
                    jp, k = divmod(g, NI)
                    stage = t * NJP + jp - 1
                    pj = (jp - 1) % NJP
                    old = a if jp == 0 else att
                    if k == 1 and old:
                        act.wait_ge(s_nmtp, stage + 1)
                        if jp == 1 and a:
                            act.wait_ge(s_dm, t)
                        copy(nmt[:, pj, :], p_n[:, 0:H]).then_inc(s_nmt, 1)
                    if g == 0 and b:
                        act.wait_ge(s_x1Tp, t - 1)
                        copy(x1T[:, :, :].rearrange("p c i -> p (c i)"), p_t).then_inc(s_x1T, 1)
                    if g == 3 and b:
                        act.wait_ge(s_hp, t - 1)
                        copy(hf[:, :], p_t[:, 0:NH]).then_inc(s_hf, 1)
                    if g == 10 and b:
                        act.wait_ge(s_hTp, t - 1)
                        copy(hT[:, :], p_n[0:NA, :]).then_inc(s_hT, 1)
                    if g == 11 and a:
                        act.wait_ge(s_wo, t)
                        copy(y0[:, :], p_t).then_inc(s_y0, 1)
                    if g == 12 and b:
                        act.wait_ge(s_y2p, t - 1)
                        copy(y20[:, :], p_t).then_inc(s_y20, 1)
                    if g == 2 and a:
                        act.wait_ge(s_dm, t)
                        A(wst[:, :, :], dm[:, :, :], ACT.Exp).then_inc(s_wst, 1)
                    if g == 5 and b:
                        act.wait_ge(s_lg, t - 1)
                        A(eg[:, :], lg[:, :], ACT.Exp, bias=nlm[:, 0:1], accum_out=gsum[:, :]).then_inc(s_eg, 1)
                    if k == 2 and old:
                        act.wait_ge(s_pv, stage + 1)
                        copy(ot[:, :, :].rearrange("p c i -> p (c i)"), pw[:, :]).then_inc(s_ot, 1)
                    if k == 3 and old:
                        act.wait_ge(s_ott, stage + 1)
                        if jp == 1 and a:
                            act.wait_ge(s_wp, t)
                        copy(parts[:, pj, :, :],
                             pw[:, :].rearrange("p (h d) -> p h d", d=32)[:, :, 0:17]).then_inc(s_part, 1)
                    if g == 0 and proj:
                        act.wait_ge(s_xTp, n + 1)
                        copy(xT[:, :, :].rearrange("p c i -> p (c i)"), pw[:, 0:2 * P]).then_inc(s_xT, 1)
                    if g == 4 and proj:
                        act.wait_ge(s_qkp, n + 1)
                        act.wait_ge(s_qks, n)
                        copy(qkf[:, :, :].rearrange("p e i -> p (e i)"), pw[:, :]).then_inc(s_qkf, 1)
                    if g == 8 and proj:
                        act.wait_ge(s_vp, n + 1)
                        act.wait_ge(s_v, n)
                        copy(vf[:, :], pw[:, 0:D]).then_inc(s_vf, 1)
                    if g == 8 and a:
                        act.wait_ge(s_oTp, t)
                        copy(oT[:, :, :].rearrange("p c i -> p (c i)"), p_t).then_inc(s_oT, 1)
                    if a if g == 0 else att:
                        before(g, t, ph)

            passes(act, tile)

        @block.vector
        def _(dve):
            v = nc.vector
            def stats(st, mv, src):
                v.bn_stats(st[:, :], src)
                dve.drain()
                return v.bn_aggr(mv[:, :], st[:, :])

            def normal(dst, src, mv, rs):
                return v.tensor_scalar(dst, src, mv[:, 0:1], rs[:, 0:1], ALU.subtract, ALU.mult)

            dve.wait_ge(s_const, N_CONST)
            stats(st0, mv0, xin[:, :]).then_inc(s_mv0, 1)
            v.tensor_scalar(w_k[:, :, :], w_k[:, :, :], HD ** -0.5, None, ALU.mult)
            v.tensor_scalar(b_qk[:, 2:4], b_qk[:, 2:4], HD ** -0.5, None, ALU.mult)
            dve.drain()
            weights = ((w_q, w_q2), (w_k, w_k2), (w_v, w_v2), (w_o, w_o2), (w_base, w_base2), (w_a, w_a2))
            for w, w2 in weights:
                v.tensor_copy(w2[:, 0, :, :], w[:, :, :])
            v.tensor_copy(w_b2[:, 0, :], w_b[:, :])
            dve.drain()
            for w, w2 in weights:
                v.tensor_tensor(w2[:, 1, :, :], w[:, :, :], w2[:, 0, :, :], ALU.subtract)
            v.tensor_tensor(w_b2[:, 1, :], w_b[:, :], w_b2[:, 0, :], ALU.subtract).then_inc(s_cdve, 1)
            dve.wait_ge(s_rs0, 1)
            normal(xn[:, :], xin[:, :], mv0, rs0).then_inc(s_xn, 1)
            v.memset(tf[:, 0:1], 0.0)
            v.tensor_copy(tf[:, 1:1 + MAX_LEN], relf[:, NREL - MAX_LEN:NREL])
            v.tensor_copy(tf[:, 1 + MAX_LEN:1 + MAX_LEN + NREL], relf[:, :])
            v.tensor_copy(tf[:, 1 + MAX_LEN + NREL:NU + 1],
                          relf[:, NREL - 1:NREL].to_broadcast((HD, NU - MAX_LEN - NREL)))
            dve.drain()
            v.tensor_copy(th[:, :], tf[:, :]).then_inc(s_tsplit, 1)
            dve.drain()
            v.tensor_tensor(tl[:, :], tf[:, :], th[:, :], ALU.subtract).then_inc(s_tsplit, 1)
            dve.wait_ge(s_cpool, 1)

            def maxima(buf, count):
                dve.wait_ge(s_scores, count)
                v.tensor_reduce(r1[:, :], sc[:, 2 * buf:2 * buf + 2, :].rearrange("p c (h i) -> p (c h) i", i=IW),
                                axis=AX.X, op=ALU.max, apply_transpose=True)
                dve.drain()
                v.tensor_tensor(r2[:, :], r1[:, 0:H], r1[:, H:2 * H], ALU.max).then_inc(s_rmax, 1)

            def spread(g, count):
                jp, i = divmod(g, NI)
                dve.wait_ge(s_maxT, count)
                part = nm[:, jp % 2, i * IW:(i + 1) * IW]
                v.tensor_reduce(part, p_max.rearrange("h (q i) -> h i q", i=IW), axis=AX.X, op=ALU.max,
                                negate=True).then_inc(s_nmr, 1)
                dve.drain()
                v.tensor_tensor(nmm[0:H, :, :], part.rearrange("h (a i) -> h a i", a=1)
                                .to_broadcast((H, H, IW)), mask_h[:, :, :], ALU.mult).then_inc(s_nm, 1)

            def side(g, t, n, proj, a, b):
                if g == 1 and a:
                    dve.wait_ge(s_nmt, t * NJP)
                    v.tensor_reduce(nmin[:, :], nmt[:, :, :].rearrange("p j h -> p h j"), axis=AX.X,
                                    op=ALU.min)
                    dve.drain()
                    v.tensor_tensor(dm[:, :, :], nmin[:, :].rearrange("p (a h) -> p a h", a=1)
                                    .to_broadcast((P, NJP, H)), nmt[:, :, :], ALU.subtract).then_inc(s_dm, 1)
                if g == 2 and proj:
                    dve.wait_ge(s_x, (n + 1) * 16)
                    stats(st0, mv0, xin[:, :]).then_inc(s_mv0, 1)
                if g == 3 and proj:
                    dve.wait_ge(s_rs0, n + 2)
                    dve.wait_ge(s_xTp, n + 1)
                    normal(xn[:, :], xin[:, :], mv0, rs0).then_inc(s_xn, 1)
                if g == 4 and b:
                    dve.wait_ge(s_hf, t - 1)
                    v.tensor_tensor(lg[:, :], hf[:, NA:NH], b_rt[:, :], ALU.add)
                    dve.drain()
                    v.tensor_reduce(nlm[:, :], lg[:, :], axis=AX.X, op=ALU.max, negate=True).then_inc(s_lg, 1)
                if g == 5 and b:
                    dve.wait_ge(s_eg, t - 1)
                    v.reciprocal(rg[:, :], gsum[:, :])
                    dve.drain()
                    v.tensor_scalar(gate[:, :], eg[:, :], rg[:, 0:1], None, ALU.mult)
                    ge = gate[:, :].rearrange("p (e a) -> p e a", a=1).to_broadcast((P, E, E))
                    gf = gate[:, :].rearrange("p (a f) -> p a f", a=1).to_broadcast((P, E, E))
                    dve.drain()
                    v.tensor_tensor(ceq[:, :, :], gf, ge, ALU.is_equal)
                    v.tensor_tensor(cgt[:, :, :], gf, ge, ALU.is_gt)
                if g == 6 and b:
                    dve.drain()
                    v.tensor_tensor(ceqt[:, :, :], ceq[:, :, :], tri[:, :, :], ALU.mult)
                    dve.drain()
                    v.tensor_tensor(cadd[:, :, :], cgt[:, :, :], ceqt[:, :, :], ALU.add)
                    dve.drain()
                    v.tensor_reduce(rank[:, :], cadd[:, :, :], axis=AX.X, op=ALU.add)
                if g == 7 and a:
                    dve.wait_ge(s_osum, t)
                    v.reciprocal(rden[:, :], osum[:, :, 16])
                    dve.drain()
                    v.tensor_tensor(o[:, :, :], osum[:, :, 0:HD], rden[:, :].rearrange("p (h a) -> p h a", a=1)
                                    .to_broadcast((P, H, HD)), ALU.mult).then_inc(s_o, 1)
                if g == 7 and b:
                    dve.drain()
                    v.scalar_tensor_tensor(out=sw[:, :], in0=rank[:, :], scalar=2.0, in1=gate[:, :],
                                           op0=ALU.is_lt, op1=ALU.mult)
                    v.tensor_copy(hw[:, 0:R], hf[:, 0:R])
                if g == 8 and b:
                    dve.drain()
                    v.tensor_reduce(ssum[:, :], sw[:, :], axis=AX.X, op=ALU.add)
                    dve.drain()
                    v.tensor_scalar(ssume[:, :], ssum[:, :], 1e-6, None, ALU.add)
                if g == 9 and b:
                    dve.drain()
                    v.reciprocal(rss[:, :], ssume[:, :])
                    dve.drain()
                    v.tensor_scalar(swn[:, :], sw[:, :], rss[:, 0:1], None, ALU.mult)
                    dve.drain()
                    v.tensor_tensor(hw[:, R:NA].rearrange("p (e r) -> p e r", r=R),
                                    hf[:, R:NA].rearrange("p (e r) -> p e r", r=R),
                                    swn[:, :].rearrange("p (e a) -> p e a", a=1).to_broadcast((P, E, R)),
                                    ALU.mult).then_inc(s_hw, 1)
                if g == 12 and a:
                    dve.wait_ge(s_y, t)
                    stats(st1, mv1, y[:, :]).then_inc(s_mv1, 1)
                if g == 13 and b:
                    dve.wait_ge(s_y2, t - 1)
                    stats(st3, mv3, y2[:, :]).then_inc(s_mv3, 1)
                if g == 13 and a:
                    dve.wait_ge(s_rs1, t)
                    normal(yn[:, :], y[:, :], mv1, rs1).then_inc(s_yn, 1)
                if g == 14 and a:
                    dve.wait_ge(s_x1, t)
                    stats(st2, mv2, x1[:, :]).then_inc(s_mv2, 1)
                if g == 14 and b:
                    dve.wait_ge(s_rs3, t - 1)
                    normal(y2n[:, :], y2[:, :], mv3, rs3).then_inc(s_y2n, 1)
                if g == 15 and a:
                    dve.wait_ge(s_rs2, t)
                    normal(xn1[:, :], x1[:, :], mv2, rs2).then_inc(s_xn1, 1)

            def tile(t, n, att, proj, a, b, ph=None):
                for g in range(NG):
                    if a if g == 0 else att:
                        spread((g - 1) % NG, t * NG + g)
                    if att:
                        maxima(buffer(ph, g), t * NG + g + 1)
                    side(g, t, n, proj, a, b)

            passes(dve, tile)


def kernel(**inputs):
    import concourse.bacc as bacc
    from concourse.bass_utils import run_bass_kernel_spmd

    def a(name):
        return np.asarray(inputs[name])

    laid = {
        "x": a("L0_attn_x").reshape(B * L, D),
        "wqT": a("L0_attn_Wq").T, "bq": a("L0_attn_bq"),
        "wkT": a("L0_attn_Wk").T, "bk": a("L0_attn_bk"),
        "wvT": a("L0_attn_Wv").T, "bv": a("L0_attn_bv"),
        "woT": a("L0_attn_Wo").T, "bo": a("L0_attn_bo"),
        "relT": a("L0_attn_rel_emb").T,
        "baseT": a("L0_ffn_base_W").T, "base_b": a("L0_ffn_base_b"),
        "shAT": a("L0_ffn_shared_A").T, "shBT": a("L0_ffn_shared_B").T,
        "roAT": a("L0_ffn_routed_A").reshape(E * R, D).T,
        "roBT": a("L0_ffn_routed_B").transpose(0, 2, 1).reshape(E * R, D),
        "rtT": a("L0_ffn_router_W").T, "rtb": a("L0_ffn_router_b"),
    }
    nc = bacc.Bacc("TRN2", target_bir_lowering=False, num_devices=1)
    arrays, aps = {}, {}
    for name, array in laid.items():
        arrays[name] = np.ascontiguousarray(array)
        aps[name] = nc.dram_tensor(name, arrays[name].shape, mybir.dt.from_np(arrays[name].dtype),
                                   kind="ExternalInput").ap()
    out = nc.dram_tensor("out", (B * L, D), mybir.dt.float32, kind="ExternalOutput").ap()
    sandwich_kernel(nc, out=out, **aps)
    r = run_bass_kernel_spmd(nc, [arrays], core_ids=[0])
    return r.results[0]["out"].reshape(B, L, D)
```
